# Optimizing a Trainium2 kernel written in Bass

```python
import numpy as np
import jax
import jax.numpy as jnp

def _softmax(x, axis=-1):
    return jax.nn.softmax(x, axis=axis)

def _gelu(x):
    return jax.nn.gelu(x, approximate=True)

def _silu(x):
    return jax.nn.silu(x)

def _sigmoid(x):
    return jax.nn.sigmoid(x)

def _layernorm(x, axis=-1, eps=1e-05):
    m = jnp.mean(x, axis=axis, keepdims=True)
    v = jnp.var(x, axis=axis, keepdims=True)
    return (x - m) / jnp.sqrt(v + eps)

def _scatter_add(tgt, idx, src, axis=0):
    return tgt.at[idx].add(src)

def _segment_sum(src, seg, n):
    return jax.ops.segment_sum(src, seg, n)
kernel_name = 'mk_prb_d1_jaxref_r8_b3a478'

def setup_inputs(seed: int=0):
    np.random.seed(seed)
    _w = jnp.asarray

    def _L0_attn_setup():
        import jax, jax.numpy as jnp
        import numpy as np
        B, N, D_MODEL, H, D_HEAD = (1, 256, 128, 16, 64)
        A0, A1, LIM = (1.0, 1.0, 1.0)

        def _fastmax_causal_p1(q, k, v):
            qn = jnp.max(jnp.linalg.norm(q, axis=-1), axis=-1)[..., None, None]
            kn = jnp.max(jnp.linalg.norm(k, axis=-1), axis=-1)[..., None, None]
            q = LIM * q / qn
            k = LIM * k / kn
            n = q.shape[2]
            kv = jnp.cumsum(k[..., :, None] * v[..., None, :], axis=2)
            num = A0 * jnp.cumsum(v, axis=2) + A1 * jnp.einsum('bhnd,bhnde->bhne', q, kv)
            ksum = jnp.cumsum(k, axis=2)
            den = A0 * jnp.arange(1, n + 1, dtype=q.dtype) + A1 * jnp.einsum('bhnd,bhnd->bhn', q, ksum)
            return num / den[..., None]
        key = jax.random.key(seed)
        ks = jax.random.split(key, 6)
        s = 1.0 / np.sqrt(D_MODEL).astype(np.float32)
        return {'X': jax.random.normal(ks[0], (B, N, D_MODEL), jnp.float32), 'Wq': jax.random.normal(ks[1], (H * D_HEAD, D_MODEL), jnp.float32) * s, 'Wk': jax.random.normal(ks[2], (H * D_HEAD, D_MODEL), jnp.float32) * s, 'Wv': jax.random.normal(ks[3], (H * D_HEAD, D_MODEL), jnp.float32) * s, 'Wo': jax.random.normal(ks[4], (D_MODEL, H * D_HEAD), jnp.float32) * s, 'bo': jnp.zeros((D_MODEL,), jnp.float32)}
    _L0_attn_in = _L0_attn_setup()

    def _L0_ffn_setup():
        import jax, jax.numpy as jnp
        import numpy as np
        NUM_EXPERTS = 8
        TOP_K = 2
        B, T, D, F = (4, 256, 128, 352)
        key = jax.random.key(seed)
        ks = jax.random.split(key, 5)
        return {'x': jax.random.normal(ks[0], (B, T, D), dtype=jnp.float32), 'router_w': jax.random.normal(ks[1], (D, NUM_EXPERTS), dtype=jnp.float32) * 0.02, 'gate_proj': jax.random.normal(ks[2], (NUM_EXPERTS, D, F), dtype=jnp.float32) * 0.02, 'up_proj': jax.random.normal(ks[3], (NUM_EXPERTS, D, F), dtype=jnp.float32) * 0.02, 'down_proj': jax.random.normal(ks[4], (NUM_EXPERTS, F, D), dtype=jnp.float32) * 0.02}
    _L0_ffn_in = _L0_ffn_setup()
    _d = {'L0_attn_X': _L0_attn_in['X'], 'L0_attn_Wq': _L0_attn_in['Wq'], 'L0_attn_Wk': _L0_attn_in['Wk'], 'L0_attn_Wv': _L0_attn_in['Wv'], 'L0_attn_Wo': _L0_attn_in['Wo'], 'L0_attn_bo': _L0_attn_in['bo'], 'L0_ffn_router_w': _L0_ffn_in['router_w'], 'L0_ffn_gate_proj': _L0_ffn_in['gate_proj'], 'L0_ffn_up_proj': _L0_ffn_in['up_proj'], 'L0_ffn_down_proj': _L0_ffn_in['down_proj']}
    _x0 = _d['L0_attn_X']
    _d['L0_attn_X'] = jax.random.normal(jax.random.fold_in(jax.random.key(seed), 1), (8, 1024, 128), dtype=_x0.dtype)
    del _x0
    return _d

def reference(L0_attn_X, L0_attn_Wq, L0_attn_Wk, L0_attn_Wv, L0_attn_Wo, L0_attn_bo, L0_ffn_router_w, L0_ffn_gate_proj, L0_ffn_up_proj, L0_ffn_down_proj):

    def _L0_attn_ref(X, Wq, Wk, Wv, Wo, bo):
        import jax, jax.numpy as jnp
        import numpy as np
        B, N, D_MODEL, H, D_HEAD = (1, 256, 128, 16, 64)
        A0, A1, LIM = (1.0, 1.0, 1.0)

        def _fastmax_causal_p1(q, k, v):
            qn = jnp.max(jnp.linalg.norm(q, axis=-1), axis=-1)[..., None, None]
            kn = jnp.max(jnp.linalg.norm(k, axis=-1), axis=-1)[..., None, None]
            q = LIM * q / qn
            k = LIM * k / kn
            n = q.shape[2]
            kv = jnp.cumsum(k[..., :, None] * v[..., None, :], axis=2)
            num = A0 * jnp.cumsum(v, axis=2) + A1 * jnp.einsum('bhnd,bhnde->bhne', q, kv)
            ksum = jnp.cumsum(k, axis=2)
            den = A0 * jnp.arange(1, n + 1, dtype=q.dtype) + A1 * jnp.einsum('bhnd,bhnd->bhn', q, ksum)
            return num / den[..., None]
        b, n, _ = X.shape

        def heads(W):
            return (X @ W.T).reshape(b, n, H, D_HEAD).transpose(0, 2, 1, 3)
        q, k, v = (heads(Wq), heads(Wk), heads(Wv))
        vh = _fastmax_causal_p1(q, k, v)
        vh = vh.transpose(0, 2, 1, 3).reshape(b, n, H * D_HEAD)
        return vh @ Wo.T + bo

    def _L0_ffn_ref(x, router_w, gate_proj, up_proj, down_proj):
        import jax, jax.numpy as jnp
        import numpy as np
        NUM_EXPERTS = 8
        TOP_K = 2
        B, T, D, F = (4, 256, 128, 352)
        scores = jnp.einsum('btd,de->bte', x, router_w).astype(jnp.float32)
        probs = jax.nn.softmax(scores, axis=-1)
        routing_weights, routing_idx = jax.lax.top_k(probs, TOP_K)
        routing_weights = (routing_weights / jnp.sum(routing_weights, axis=-1, keepdims=True)).astype(x.dtype)
        one_hot = jax.nn.one_hot(routing_idx, NUM_EXPERTS, dtype=x.dtype)
        expert_w = jnp.einsum('btke,btk->bte', one_hot, routing_weights)
        dispatched = jnp.einsum('btd,btke->bted', x, one_hot)
        gate = jnp.einsum('bted,edf->btef', dispatched, gate_proj)
        up = jnp.einsum('bted,edf->btef', dispatched, up_proj)
        acts = jax.nn.silu(gate) * up
        expert_out = jnp.einsum('btef,efd->bted', acts, down_proj)
        return jnp.einsum('bted,bte->btd', expert_out, expert_w)
    x = L0_attn_X
    xn = _layernorm(x, axis=-1)
    x = x + _L0_attn_ref(xn, L0_attn_Wq, L0_attn_Wk, L0_attn_Wv, L0_attn_Wo, L0_attn_bo) + _L0_ffn_ref(xn, L0_ffn_router_w, L0_ffn_gate_proj, L0_ffn_up_proj, L0_ffn_down_proj)
    return x

_drawn_inputs = setup_inputs


def setup_inputs(seed=0):
    import zlib

    import numpy as np

    out = dict(_drawn_inputs(seed))
    spreads = {'L0_attn_bo': (0.0, 0.42)}
    factors = {'L0_ffn_router_w': 8.0,
     'L0_ffn_gate_proj': 8.0,
     'L0_ffn_up_proj': 8.0,
     'L0_ffn_down_proj': 8.0,
     'L0_attn_Wq': 8.0,
     'L0_attn_Wk': 8.0}
    for name, (base, spread) in spreads.items():
        noise = np.random.default_rng([zlib.crc32(name.encode()), seed]).standard_normal(out[name].shape)
        drawn = base * np.exp(spread * noise) if base else spread * noise
        out[name] = jnp.asarray(drawn.astype(out[name].dtype))
    for name, factor in factors.items():
        out[name] = (out[name] * factor).astype(out[name].dtype)
    return out
```

```python
import concourse.bass as bass
from concourse import mybir
from contextlib import ExitStack

B, N, D = 8, 1024, 128
H, DH = 16, 64
E, F = 8, 352
P = 128
C = B * N // P
CB = N // P
Q, HQ = 4, H // 4
W4 = HQ * P
VE = DH + 2
K2 = 2
TILES = K2 * C + E
SLOTS = (TILES + 1) * P
FT = [(0, 128), (128, 128), (256, 96)]
AHEAD = 2
EPS = 1e-5


def build(nc, x, wq, wk, wv, wo, bo, rw, gate, up, down, out):
    f32, f32r, bf16 = mybir.dt.float32, mybir.dt.float32r, mybir.dt.bfloat16
    i32, u32 = mybir.dt.int32, mybir.dt.uint32
    ALU, ACT, AX = mybir.AluOpType, mybir.ActivationFunctionType, mybir.AxisListType

    xs_d = nc.dram_tensor("sorted_tokens", (SLOTS, D), f32, kind="Internal").ap()
    ys_d = nc.dram_tensor("expert_rows", (SLOTS, D), f32, kind="Internal").ap()

    ctx = ExitStack()
    with ctx:
        at = [nc.sbuf_base]

        def place(name, shape, dt=f32, size=4):
            n = size
            for d in shape[1:]:
                n *= d
            t = nc.alloc_sbuf_tensor_at(name, shape, dt, offset=at[0])
            at[0] += -(-n // 32) * 32
            return t

        at[0] = -(-at[0] // 32) * 32
        xa = place("xa", [P, C + 1, D])
        mv = place("mv", [P, C, 2])
        rstd = place("rstd", [P, C + 1])
        nmr = place("nmr", [P, C + 1])
        nmr1 = place("nmr1", [P, C + 1])
        wmean = place("wmean", [P, 3, 8])
        t64 = place("t64", [P, 2, C])
        xn = place("xn", [P, 2, D + 2])
        xTh, xTl = place("xTh", [P, 2, P], f32r), place("xTl", [P, 2, P], f32r)
        ident = place("ident", [P, P])
        causal = place("causal", [P, P])
        before = place("before", [P, P], bf16, 2)
        ones = place("ones", [P, P], bf16, 2)
        onesf = place("onesf", [P, P])
        zeros = place("zeros", [P, D])
        bob = place("bob", [P, D])
        Mf = place("Mf", [P, H, D])
        Mh, Ml = place("Mh", [P, H, D], f32r), place("Ml", [P, H, D], f32r)
        Mt = place("Mt", [P, HQ, D])
        Wvh, Wvl = place("Wvh", [P, H * DH], f32r), place("Wvl", [P, H * DH], f32r)
        WoT = place("WoT", [P, 8, D])
        cc = place("cc", [P, B, H])
        slot = place("slot", [P, K2 * C], i32)
        wtop = place("wtop", [P, K2, C])
        pad = place("pad", [P, E], i32)
        tile_e = place("tile_e", [P, TILES], i32)
        sidx = place("sidx", [P, 4], i32)
        shared = at[0]
        WNh, WNl = place("WNh", [P, 2 * H * DH], f32r), place("WNl", [P, 2 * H * DH], f32r)
        rwf, rwh, rwl = place("rwf", [P, E]), place("rwh", [P, E], f32r), place("rwl", [P, E], f32r)
        wqn, wkn, wvn, won = (place(n, [P, 8, D]) for n in ("wqn", "wkn", "wvn", "won"))
        sq = place("sq", [P, 4, 512])
        ssq = place("ssq", [P, C, 2 * H])
        mx = place("mx", [P, B, 2 * H])
        mxa = place("mxa", [P, B, 2 * H])
        ra, rb = place("ra", [P, B, 2 * H]), place("rb", [P, B, 2 * H])
        L = place("L", [P, C, E])
        L2 = place("L2", [P, C, E])
        eqw = place("eqw", [P, C, E])
        oh = place("oh", [P, K2, C, E])
        ohb = place("ohb", [P, K2, C, E], bf16, 2)
        pre = place("pre", [P, K2 * C, E])
        posn = place("posn", [P, K2 * C, E])
        slf = place("slf", [P, K2 * C])
        m1, m2, mm = place("m1", [P, C]), place("m2", [P, C]), place("mm", [P, C])
        ord8 = place("ord8", [P, E])
        cnt, til, endt, base = (place(n, [P, E]) for n in ("cnt", "til", "endt", "base"))
        cnti = place("cnti", [P, E], i32)
        iot = place("iot", [P, TILES])
        iop = place("iop", [P, 1])
        ge = place("ge", [P, TILES, E])
        tef = place("tef", [P, TILES])
        padf = place("padf", [P, E])
        end1 = at[0]
        at[0] = shared
        uh, ul = place("uh", [P, Q, HQ, P], f32r), place("ul", [P, Q, HQ, P], f32r)
        Am = place("Am", [P, Q, HQ, P])
        vx = place("vx", [P, 2, H, VE])
        Th, Tl = place("Th", [P, 2, H, VE], f32r), place("Tl", [P, 2, H, VE], f32r)
        Gf = place("Gf", [P, D + 2])
        Gh, Gl = place("Gh", [P, D + 2], f32r), place("Gl", [P, D + 2], f32r)
        rden = place("rden", [P, Q, HQ])
        nn = place("nn", [P, Q, HQ, DH])
        nT = place("nT", [P, Q, 2, P])
        end2 = at[0]
        at[0] = shared
        guf = place("guf", [P, 2, F])
        dnf = place("dnf", [P, 3, D])
        guh, gul = place("guh", [P, E, 2, F], f32r), place("gul", [P, E, 2, F], f32r)
        dnh, dnl = place("dnh", [P, E, 3, D], f32r), place("dnl", [P, E, 3, D], f32r)
        xt = place("xt", [P, 2, D])
        xtTh, xtTl = place("xtTh", [P, 2, P], f32r), place("xtTl", [P, 2, P], f32r)
        sl = place("sl", [P, 2, F])
        act_ = place("act_", [P, 2, F])
        aTh, aTl = place("aTh", [P, 2, 3, P], f32r), place("aTl", [P, 2, 3, P], f32r)
        yt = place("yt", [P, 2, D])
        gx = place("gx", [P, 2, K2, D])
        ot = place("ot", [P, 2, D])
        assert max(end1, end2, at[0]) <= nc.sbuf_usable_end, (end1, end2, at[0])

        bank = [ctx.enter_context(nc.psum_tensor(f"bank{n}", [P, 512], f32)) for n in range(8)]

        sems = {}

        def sem(name):
            sems[name] = ctx.enter_context(nc.semaphore(name))
            return sems[name]

        phase = sem("phase")
        s_pass = sem("s_pass")
        x_in, w_in, bo_in = [sem(f"x_in{n}") for n in range(8)], [sem(f"w_in{n}") for n in range(5)], sem("bo_in")
        s_ctr = sem("s_ctr")
        s_const, s_pool = sem("s_const"), sem("s_pool")
        s_tr, s_trh, s_trl = sem("s_tr"), sem("s_trh"), sem("s_trl")
        s_stat, s_chain, s_rt, s_sqrt = sem("s_stat"), sem("s_chain"), sem("s_rt"), sem("s_sqrt")
        n_xn, n_xT, n_xTh, n_xTl = sem("n_xn"), sem("n_xT"), sem("n_xTh"), sem("n_xTl")
        n_qk, n_sq, n_red, n_lg, n_lc = sem("n_qk"), sem("n_sq"), sem("n_red"), sem("n_lg"), sem("n_lc")
        s_mx, s_all = sem("s_mx"), sem("s_all")
        r_oh, r_cnt = sem("r_oh"), sem("r_cnt")
        z_tail, z_out, c_xn, c_idx = sem("z_tail"), sem("z_out"), sem("c_xn"), sem("c_idx")
        c_out = [sem("c_out0"), sem("c_out1")]
        a_u, a_v, a_s, a_T, a_G, a_xT, a_num, a_nT, a_y = (
            sem(f"a_{n}") for n in ("u", "v", "s", "T", "G", "xT", "num", "nT", "y"))
        e_uh, e_ul, e_v, e_A, e_Th, e_Tl, e_G, e_xn, e_xTh, e_xTl, e_nn, e_nT, e_y, e_M, e_r = (
            sem(f"e_{n}") for n in
            ("uh", "ul", "v", "A", "Th", "Tl", "G", "xn", "xTh", "xTl", "nn", "nT", "y", "M", "r"))
        s_Mt, s_Mh = sem("s_Mt"), sem("s_Mh")
        s_gh, s_gl, e_Gs, s_new = sem("s_gh"), sem("s_gl"), sem("e_Gs"), sem("s_new")
        f_w, f_wh, f_wl = sem("f_w"), sem("f_wh"), sem("f_wl")
        f_xt, f_out = [sem("f_xt0"), sem("f_xt1")], [sem("f_out0"), sem("f_out1")]
        f_xT, f_xTh, f_xTl = sem("f_xT"), sem("f_xTh"), sem("f_xTl")
        f_g, f_u, f_sl, f_act, f_aT, f_aTh, f_aTl, f_y, f_yt = (
            sem(f"f_{n}") for n in ("g", "u", "sl", "act", "aT", "aTh", "aTl", "y", "yt"))
        o_idx, o_c, o_b = (sem(f"o_{n}") for n in ("idx", "c", "b"))
        o_g, o_out = [sem("o_g0"), sem("o_g1")], [sem("o_out0"), sem("o_out1")]
        o_h = sem("o_h")

        def ev(n, c, k=0):
            return n * (c + AHEAD) + k + 1

        def start_ahead(eng, *pairs):
            for s, n in pairs:
                eng.sem_inc(s, n * AHEAD)

        def barrier(eng, n):
            eng.drain().then_inc(phase, 1)
            eng.wait_ge(phase, 5 * n)

        JOBS = ["u0", "u1", "v0", "s0", "v1", "u2", "s1", "T0", "u3", "s2", "T1", "s3", "G", "xT"]
        FREED = {"u": (e_ul, 4), "v": (e_v, 2), "s": (e_A, 4), "T": (e_Tl, 2),
                 "G": (e_G, 1), "x": (e_xTl, 1)}

        def wide(par, job):
            return bank[(len(JOBS) * par + JOBS.index(job)) % 4]

        def wait_wide(eng, c, job):
            j = JOBS.index(job) - 4
            who = JOBS[j]
            s, n = FREED[who[0]]
            k = int(who[1]) if who[1:].isdigit() else 0
            late = (j < 0) - (who == "xT")
            eng.wait_ge(s, ev(n, c - late, k))

        SETUP = ([("M", n) for n in range(4)] + [("q", n) for n in range(2)] +
                 [("k", n) for n in range(2)] + [("v", n) for n in range(2)] +
                 [("o", n) for n in range(2)])

        block = ctx.enter_context(nc.Block())

        @block.sync
        def _(sp):
            for n, (t, src) in enumerate(((wqn, wq), (wkn, wk), (wvn, wv))):
                sp.dma_start(t[:], src.rearrange("(t p) d -> p t d", p=P)).then_inc(w_in[n], 16)
            for n in range(8):
                sp.dma_start(xa[:, n * CB:(n + 1) * CB, :],
                             x[n].rearrange("(c p) d -> p c d", p=P)).then_inc(x_in[n], 16)
            sp.dma_start(won[:], wo.rearrange("o (t d) -> o t d", d=D)).then_inc(w_in[3], 16)
            sp.dma_start(rwf[:], rw).then_inc(w_in[4], 16)
            sp.dma_start(bob[:], bo.rearrange("(a d) -> a d", a=1).broadcast_to([P, D])).then_inc(bo_in, 16)
            sp.wait_ge(s_pool, 1)
            sp.dma_start(xs_d[(K2 * C + 1) * P:SLOTS, :].rearrange("(t p) d -> p t d", p=P),
                         zeros[:].rearrange("p (t d) -> p t d", t=1).broadcast_to([P, E, D])).then_inc(z_tail, 16)
            sp.wait_ge(bo_in, 16)
            sp.dma_start(ys_d[0:P, :], zeros[:]).then_inc(z_tail, 16)
            sp.wait_ge(z_tail, 32)
            barrier(sp, 1)
            barrier(sp, 2)
            for e in range(E):
                if e:
                    sp.wait_ge(f_wl, 2 * e)
                sp.dma_start(guf[:, 0, :], gate[e]).then_inc(f_w, 16)
                sp.dma_start(guf[:, 1, :], up[e]).then_inc(f_w, 16)
                sp.dma_start(dnf[:, 0:2, :], down[e, 0:256, :].rearrange("(t p) d -> p t d", p=P)).then_inc(f_w, 16)
                sp.dma_start(dnf[0:96, 2, :], down[e, 256:F, :]).then_inc(f_w, 16)
            with sp.Fori(0, TILES // 2) as i2:
                for s in range(2):
                    i = i2 * 2 + s
                    sp.wait_ge(f_xT, ev(1, i - 2))
                    sp.dma_start(xt[:, s, :], xs_d[bass.ds((i + 1) * P, P), :]).then_inc(f_xt[s], 16)
            barrier(sp, 3)
            with sp.Fori(0, C // 2) as c2:
                for s in range(2):
                    c = c2 * 2 + s
                    sp.wait_ge(o_b, ev(1, c))
                    sp.dma_start(out[bass.ds(c, 1)].rearrange("a p d -> p (a d)"), ot[:, s, :]).then_inc(o_out[s], 16)
            for s in range(2):
                sp.wait_ge(o_out[s], 16 * (C // 2 + 1))

        @block.gpsimd
        def _(pool):
            start_ahead(pool, (e_M, 4), (o_b, 1), *((t, 8) for t in f_out + o_out))
            pool.memset(zeros[:], 0.0).then_inc(s_pool, 1)
            pool.memset(ident[:], 0.0).then_inc(s_pool, 1)
            pool.memset(causal[:], 1.0).then_inc(s_pool, 1)
            pool.memset(onesf[:], 1.0).then_inc(s_pool, 1)
            pool.memset(before[:], 1.0).then_inc(s_pool, 1)
            pool.memset(ones[:], 1.0).then_inc(s_pool, 1)
            pool.memset(xn[:, :, D:D + 2], 1.0).then_inc(s_pool, 1)
            pool.memset(xa[:, C, :], 0.0).then_inc(s_pool, 1)
            pool.memset(rstd[:, C:C + 1], 0.0).then_inc(s_pool, 1)
            pool.memset(nmr[:, C:C + 1], 0.0).then_inc(s_pool, 1)
            pool.memset(nmr1[:, C:C + 1], 0.0).then_inc(s_pool, 1)
            pool.wait_ge(s_pool, 11)
            pool.affine_select(out=ident[:], in_=ident[:], compare_op=ALU.not_equal, fill=1.0,
                               base=0, pattern=[[-1, P]], channel_multiplier=1).then_inc(s_const, 1)
            pool.affine_select(out=causal[:], in_=causal[:], compare_op=ALU.is_ge, fill=0.0,
                               base=0, pattern=[[1, P]], channel_multiplier=-1).then_inc(s_const, 1)
            pool.affine_select(out=before[:], in_=before[:], compare_op=ALU.is_gt, fill=0.0,
                               base=0, pattern=[[1, P]], channel_multiplier=-1).then_inc(s_const, 1)
            pool.iota(ord8[:], pattern=[[-1, E]], base=E, channel_multiplier=0,
                      allow_small_or_imprecise_dtypes=True).then_inc(s_const, 1)
            pool.iota(iot[:], pattern=[[1, TILES]], base=0, channel_multiplier=0,
                      allow_small_or_imprecise_dtypes=True).then_inc(s_const, 1)
            pool.iota(iop[:], pattern=[[0, 1]], base=0, channel_multiplier=1,
                      allow_small_or_imprecise_dtypes=True).then_inc(s_const, 1)
            pool.wait_ge(s_mx, 1)
            pool.partition_all_reduce(mxa[:].rearrange("p b h -> p (b h)"), mx[:].rearrange("p b h -> p (b h)"),
                                      P, bass.bass_isa.ReduceOp.max).then_inc(s_all, 1)
            barrier(pool, 1)

            for e in range(E):
                pool.indirect_dma_start(xs_d, bass.IndirectOffsetOnAxis(ap=pad[:, e:e + 1], axis=0),
                                        zeros[:], None).then_inc(z_out, 16)
            pool.wait_ge(z_out, 16 * E)
            def scatter(c, s, first):
                if first is not None:
                    pool.wait_ge(c_out[s], 16 * K2 * first)
                    pool.sem_inc(s_pass, 1)
                for k in range(K2):
                    pool.tensor_copy(sidx[:, 2 * s + k:2 * s + k + 1],
                                     slot[:, bass.ds(c + k * C, 1)]).then_inc(c_idx, 1)
                pool.wait_ge(c_idx, K2 * c + K2)
                pool.wait_ge(c_xn, c + 1)
                pool.sem_inc(s_pass, 1)
                for k in range(K2):
                    pool.indirect_dma_start(
                        xs_d, bass.IndirectOffsetOnAxis(ap=sidx[:, 2 * s + k:2 * s + k + 1], axis=0),
                        xn[:, s, 0:D], None).then_inc(c_out[s], 16)

            for s in range(2):
                scatter(s, s, None)
            with pool.Fori(1, C // 2) as c2:
                for s in range(2):
                    scatter(c2 * 2 + s, s, c2)
            for s in range(2):
                pool.wait_ge(c_out[s], 16 * K2 * (C // 2))

            with pool.Fori(0, B) as b:
                for q in range(Q):
                    hs = slice(HQ * q, HQ * q + HQ)
                    pool.tensor_tensor(Mt[:], Mf[:, hs, :],
                                       cc[:, bass.ds(b, 1), hs].rearrange("p a h -> p (a h)").unsqueeze(2).broadcast_to([P, HQ, D]),
                                       ALU.mult).then_inc(s_Mt, 1)
                    pool.wait_ge(s_Mt, 4 * b + q + 1)
                    pool.wait_ge(a_u, ev(4, CB * b - 1, q))
                    pool.sem_inc(s_pass, 1)
                    pool.tensor_copy(Mh[:, hs, :], Mt[:]).then_inc(s_Mh, 1)
                    pool.wait_ge(s_Mh, 4 * b + q + 1)
                    pool.tensor_tensor(Ml[:, hs, :], Mt[:], Mh[:, hs, :], ALU.subtract).then_inc(e_M, 1)
                    pool.wait_ge(e_M, 4 * b + q + 1 + 4 * AHEAD)
            barrier(pool, 2)
            barrier(pool, 3)
            with pool.Fori(0, C // 2) as c2:
                for s in range(2):
                    c = c2 * 2 + s
                    pool.wait_ge(o_c, ev(1, c - 2))
                    pool.sem_inc(s_pass, 1)
                    for k in range(K2):
                        pool.tensor_copy(sidx[:, 2 * s + k:2 * s + k + 1],
                                         slot[:, bass.ds(c + k * C, 1)]).then_inc(o_idx, 1)
                    pool.wait_ge(o_idx, 2 * c + 2)
                    pool.sem_inc(s_pass, 1)
                    for k in range(K2):
                        pool.indirect_dma_start(
                            gx[:, s, k, :], None, ys_d,
                            bass.IndirectOffsetOnAxis(ap=sidx[:, 2 * s + k:2 * s + k + 1], axis=0)).then_inc(o_g[s], 16)
                    pool.wait_ge(o_c, ev(1, c))
                    pool.tensor_tensor(ot[:, s, :], ot[:, s, :], bob[:], ALU.add).then_inc(o_b, 1)

        @block.scalar
        def _(act):
            start_ahead(act, (n_xn, 1), (n_xTh, 1), (n_sq, 4), (e_uh, 4), (e_v, 2), (e_Th, 2),
                        (e_xn, 1), (e_xTh, 1), (e_nT, 4), (f_xTh, 1), (f_sl, 1), (f_aTh, 1), (f_yt, 1))
            place_of = {"q": (WNh, 0), "k": (WNh, 1024), "v": (Wvh, 0)}
            for j, (kind, n) in enumerate(SETUP):
                act.wait_ge(s_tr, j + 1)
                b_ = bank[j % 4]
                if kind == "M":
                    h0 = 8 * (n // 2) + n % 2
                    dst = Mf[:, h0:h0 + 7:2, :]
                    src = b_[:].rearrange("p (h d) -> p h d", d=D)
                elif kind == "o":
                    dst = WoT[:, 4 * n:4 * n + 4, :]
                    src = b_[:].rearrange("p (h d) -> p h d", d=D)
                else:
                    t, o = place_of[kind]
                    dst, src = t[:, o + 512 * n:o + 512 * n + 512], b_[:]
                act.activation(dst, src, ACT.Copy).then_inc(s_trh, 1)
            act.wait_ge(w_in[4], 16)
            act.activation(rwh[:], rwf[:], ACT.Copy).then_inc(s_trh, 1)
            act.wait_ge(s_stat, 1)
            act.activation(t64[:, 1, :], t64[:, 0, :], ACT.Sqrt).then_inc(s_sqrt, 1)
            act.wait_ge(s_stat, 2)
            act.wait_ge(s_pool, 11)

            with act.Fori(0, C // 2) as c2:
                for s in range(2):
                    c = c2 * 2 + s
                    act.wait_ge(n_xT, ev(1, c - 2))
                    act.activation(xn[:, s, 0:D], xa[:, bass.ds(c, 1), :].rearrange("p a d -> p (a d)"), ACT.Identity,
                                   scale=rstd[:, bass.ds(c, 1)], bias=nmr[:, bass.ds(c, 1)]).then_inc(n_xn, 1)
                    act.wait_ge(n_xT, ev(1, c))
                    act.wait_ge(n_lg, ev(1, c - 2))
                    act.activation(xTh[:, s, :], bank[4 + s][:, 0:P], ACT.Copy).then_inc(n_xTh, 1)
                    for j in range(4):
                        act.wait_ge(n_qk, ev(4, c, j))
                        act.wait_ge(n_red, ev(4, c - 1, j))
                        act.activation(sq[:, j, :], bank[j][:], ACT.Square).then_inc(n_sq, 1)
            act.wait_ge(s_all, 1)
            act.activation(ra[:], mxa[:], ACT.Sqrt).then_inc(s_sqrt, 1)
            act.wait_ge(s_rt, 1)
            act.activation(mm[:], mm[:], ACT.Exp).then_inc(s_sqrt, 1)
            barrier(act, 1)

            def for_scatter(c, s):
                act.activation(xn[:, s, 0:D], xa[:, bass.ds(c, 1), :].rearrange("p a d -> p (a d)"), ACT.Identity,
                               scale=rstd[:, bass.ds(c, 1)], bias=nmr[:, bass.ds(c, 1)]).then_inc(c_xn, 1)

            for s in range(2):
                for_scatter(s, s)
            with act.Fori(1, C // 2) as c2:
                for s in range(2):
                    act.wait_ge(c_out[s], 16 * K2 * c2)
                    for_scatter(c2 * 2 + s, s)
            for s in range(2):
                act.wait_ge(c_out[s], 16 * K2 * (C // 2))

            def normalise(c, s):
                act.wait_ge(a_G, ev(1, c - 2))
                act.activation(xn[:, s, 0:D], xa[:, bass.ds(c, 1), :].rearrange("p a d -> p (a d)"), ACT.Identity,
                               scale=rstd[:, bass.ds(c, 1)], bias=nmr1[:, bass.ds(c, 1)]).then_inc(e_xn, 1)

            def transposed(c, s, job_par):
                act.wait_ge(a_xT, ev(1, c))
                act.activation(xTh[:, s, :], wide(job_par, "xT")[:, 0:P], ACT.Copy).then_inc(e_xTh, 1)

            def u_out(c, s, q):
                act.wait_ge(a_u, ev(4, c, q))
                act.wait_ge(a_num, ev(4, c - 1, q))
                act.activation(uh[:, q].rearrange("p h i -> p (h i)"), wide(s, f"u{q}")[:], ACT.Identity,
                               bias=1.0 / D).then_inc(e_uh, 1)

            def v_out(c, s, n):
                act.wait_ge(a_v, ev(2, c, n))
                act.wait_ge(a_num, ev(4, c - 2, 3))
                act.activation(vx[:, s, 8 * n:8 * n + 8, 0:DH],
                               wide(s, f"v{n}")[:].rearrange("p (h e) -> p h e", e=DH), ACT.Copy).then_inc(e_v, 1)

            def T_out(c, s, n):
                act.wait_ge(a_T, ev(2, c, n))
                act.wait_ge(a_num, ev(4, c - 2, 3))
                act.activation(Th[:, s, 8 * n:8 * n + 8, 0:DH],
                               wide(s, f"T{n}")[:].rearrange("p (h e) -> p h e", e=DH), ACT.Copy).then_inc(e_Th, 1)

            def nT_out(c, q):
                act.wait_ge(a_nT, ev(4, c, q))
                act.wait_ge(a_y, ev(1, c - 1))
                act.activation(nT[:, q].rearrange("p t i -> p (t i)"), bank[6][:, 0:2 * P], ACT.Copy).then_inc(e_nT, 1)

            normalise(0, 0)
            transposed(0, 0, 1)
            with act.Fori(0, C // 2) as c2:
                for s in range(2):
                    c = c2 * 2 + s
                    u_out(c, s, 0)
                    u_out(c, s, 1)
                    v_out(c, s, 0)
                    normalise(c + 1, 1 - s)
                    v_out(c, s, 1)
                    u_out(c, s, 2)
                    T_out(c, s, 0)
                    u_out(c, s, 3)
                    T_out(c, s, 1)
                    nT_out(c, 0)
                    transposed(c + 1, 1 - s, s)
                    for q in range(1, Q):
                        nT_out(c, q)
            barrier(act, 2)

            for e in range(E):
                act.wait_ge(f_w, 64 * (e + 1))
                act.activation(guh[:, e], guf[:], ACT.Copy).then_inc(f_wh, 1)
                act.activation(dnh[:, e, 0:2, :], dnf[:, 0:2, :], ACT.Copy).then_inc(f_wh, 1)
                act.activation(dnh[0:96, e, 2, :], dnf[0:96, 2, :], ACT.Copy).then_inc(f_wh, 1)
            act.preload_act_table(ACT.Silu)
            with act.Fori(0, TILES // 2) as i2:
                for s in range(2):
                    i = i2 * 2 + s
                    act.wait_ge(f_xT, ev(1, i))
                    act.wait_ge(f_u, ev(1, i - 2))
                    act.activation(xtTh[:, s, :], bank[0][:, 0:P], ACT.Copy).then_inc(f_xTh, 1)
                    act.wait_ge(f_g, ev(1, i))
                    act.wait_ge(f_act, ev(1, i - 2))
                    act.activation(sl[:, s, :], bank[1 + s][:, 0:F], ACT.Silu).then_inc(f_sl, 1)
                    act.wait_ge(f_aT, ev(1, i))
                    act.wait_ge(f_y, ev(1, i - 2))
                    act.activation(aTh[:, s, 0:2, :], bank[5][:, 0:2 * P].rearrange("p (t i) -> p t i", t=2), ACT.Copy)
                    act.activation(aTh[0:96, s, 2, :], bank[5][0:96, 2 * P:3 * P], ACT.Copy).then_inc(f_aTh, 1)
                    act.wait_ge(f_y, ev(1, i))
                    act.wait_ge(f_out[s], 16 * i2 + 16)
                    act.activation(yt[:, s, :], bank[6 + s][:, 0:D], ACT.Copy).then_inc(f_yt, 1)
                    act.wait_ge(f_yt, ev(1, i))
                    act.dma_start(ys_d[bass.ds((i + 1) * P, P), :], yt[:, s, :]).then_inc(f_out[s], 16)
            for s in range(2):
                act.wait_ge(f_out[s], 16 * (TILES // 2 + 1))
            barrier(act, 3)

        @block.vector
        def _(dve):
            start_ahead(dve, (n_xTl, 1), (n_red, 4), (n_lc, 1), (e_ul, 4), (e_A, 4), (e_Tl, 2), (e_G, 1),
                        (e_xTl, 1), (e_nn, 4), (e_y, 1), (e_r, 4), (f_xTl, 1), (f_act, 1), (f_aTl, 1), (o_c, 1))
            links = [0]

            def link(ins):
                links[0] += 1
                ins.then_inc(s_chain, 1)
                dve.wait_ge(s_chain, links[0])

            def rsqrt(dst, val, root, tmp):
                link(dve.reciprocal(dst, root))
                link(dve.tensor_tensor(tmp, dst, dst, ALU.mult))
                link(dve.tensor_tensor(tmp, tmp, val, ALU.mult))
                link(dve.tensor_scalar(tmp, tmp, -0.5, 1.5, ALU.mult, ALU.add))
                link(dve.tensor_tensor(dst, dst, tmp, ALU.mult))

            for n, t in enumerate((wqn, wkn, wvn)):
                dve.wait_ge(w_in[n], 16)
                link(dve.tensor_reduce(wmean[:, n, :], t[:], AX.X, ALU.add))
                link(dve.tensor_scalar(wmean[:, n, :], wmean[:, n, :], 1.0 / D, None, ALU.mult))
                dve.tensor_tensor(t[:], t[:], wmean[:, n, :].unsqueeze(2).broadcast_to([P, 8, D]),
                                  ALU.subtract).then_inc(s_ctr, 1)
            for n in range(B):
                dve.wait_ge(x_in[n], 16)
                for c in range(n * CB, n * CB + CB):
                    link(dve.bn_stats(eqw[:, c, 0:6], xa[:, c, :]))
                    link(dve.bn_aggr(mv[:, c, :], eqw[:, c, 0:6]))
            dve.tensor_scalar(t64[:, 0, :], mv[:, :, 1], EPS, None, ALU.add).then_inc(s_stat, 1)
            place_of = {"q": (WNl, WNh, 0), "k": (WNl, WNh, 1024), "v": (Wvl, Wvh, 0)}
            for j, (kind, n) in enumerate(SETUP):
                if kind in place_of:
                    lo, hi, o = place_of[kind]
                    dve.wait_ge(s_trh, j + 1)
                    dve.tensor_tensor(lo[:, o + 512 * n:o + 512 * n + 512], bank[j % 4][:],
                                      hi[:, o + 512 * n:o + 512 * n + 512], ALU.subtract).then_inc(s_trl, 1)
            dve.wait_ge(s_trh, len(SETUP) + 1)
            dve.tensor_tensor(rwl[:], rwf[:], rwh[:], ALU.subtract).then_inc(s_trl, 1)
            dve.wait_ge(s_sqrt, 1)
            rsqrt(rstd[:, 0:C], t64[:, 0, :], t64[:, 1, :], mm[:])
            dve.scalar_tensor_tensor(nmr[:, 0:C], mv[:, :, 0], -1.0, rstd[:, 0:C], ALU.mult, ALU.mult).then_inc(s_stat, 1)
            dve.wait_ge(s_stat, 2)
            dve.tensor_scalar(nmr1[:, 0:C], nmr[:, 0:C], 1.0, None, ALU.add).then_inc(s_stat, 1)

            with dve.Fori(0, C // 2) as c2:
                for s in range(2):
                    c = c2 * 2 + s
                    dve.wait_ge(n_xTh, ev(1, c))
                    dve.tensor_tensor(xTl[:, s, :], bank[4 + s][:, 0:P], xTh[:, s, :], ALU.subtract).then_inc(n_xTl, 1)
                    for j in range(4):
                        dve.wait_ge(n_sq, ev(4, c, j))
                        dve.tensor_reduce(ssq[:, bass.ds(c, 1), 8 * j:8 * j + 8].rearrange("p a h -> p (a h)"),
                                          sq[:, j, :].rearrange("p (h e) -> p h e", e=DH),
                                          AX.X, ALU.add).then_inc(n_red, 1)
                    dve.wait_ge(n_lg, ev(1, c))
                    dve.tensor_copy(L[:, bass.ds(c, 1), :].rearrange("p a e -> p (a e)"), bank[6 + s][:, 0:E]).then_inc(n_lc, 1)
            dve.wait_ge(n_red, ev(4, C - 1, 3))
            dve.wait_ge(n_lc, ev(1, C - 1))
            dve.tensor_reduce(mx[:], ssq[:].rearrange("p (b c) h -> p b h c", b=B), AX.X, ALU.max).then_inc(s_mx, 1)

            bc = [P, C, E]
            link(dve.tensor_reduce(m1[:], L[:], AX.X, ALU.max))

            def first_of(best, src, k):
                link(dve.tensor_tensor(eqw[:], src[:], best[:].unsqueeze(2).broadcast_to(bc), ALU.is_equal))
                link(dve.tensor_tensor(eqw[:], eqw[:], ord8[:].unsqueeze(1).broadcast_to(bc), ALU.mult))
                link(dve.tensor_reduce(slf[:, 0:C], eqw[:], AX.X, ALU.max))
                link(dve.tensor_tensor(oh[:, k], ord8[:].unsqueeze(1).broadcast_to(bc),
                                       slf[:, 0:C].unsqueeze(2).broadcast_to(bc), ALU.is_equal))
                dve.tensor_copy(ohb[:, k], oh[:, k]).then_inc(r_oh, 1)

            dve.wait_ge(s_const, 6)
            first_of(m1, L, 0)
            link(dve.scalar_tensor_tensor(L2[:].rearrange("p c e -> p (c e)"),
                                          oh[:, 0].rearrange("p c e -> p (c e)"), -3.0e38,
                                          L[:].rearrange("p c e -> p (c e)"), ALU.mult, ALU.add))
            link(dve.tensor_reduce(m2[:], L2[:], AX.X, ALU.max))
            first_of(m2, L2, 1)
            dve.tensor_tensor(mm[:], m2[:], m1[:], ALU.subtract).then_inc(s_rt, 1)
            dve.wait_ge(s_sqrt, 3)
            link(dve.tensor_scalar(m1[:], mm[:], 1.0, None, ALU.add))
            link(dve.reciprocal(wtop[:, 0, :], m1[:]))
            link(dve.tensor_tensor(wtop[:, 1, :], wtop[:, 0, :], mm[:], ALU.mult))
            rsqrt(rb[:], mxa[:], ra[:], mx[:])
            link(dve.tensor_tensor(cc[:], rb[:, :, 0:H], rb[:, :, H:2 * H], ALU.mult))
            dve.wait_ge(r_cnt, 1)
            for k in range(K2):
                for e in range(E):
                    first = 0.0 if k == 0 else pre[:, C - 1, e:e + 1]
                    link(dve.tensor_tensor_scan(pre[:, k * C:(k + 1) * C, e], onesf[:, 0:C],
                                                bank[2 + k][:].rearrange("p (c e) -> p c e", e=E)[:, :, e],
                                                first, ALU.mult, ALU.add))
            link(dve.tensor_copy(cnt[:], pre[:, K2 * C - 1, :]))
            link(dve.tensor_scalar(til[:], cnt[:], float(P - 1), None, ALU.add))
            link(dve.tensor_copy(cnti[:], til[:]))
            link(dve.tensor_single_scalar(cnti[:], cnti[:], 7, ALU.logical_shift_right))
            link(dve.tensor_copy(til[:], cnti[:]))
            link(dve.tensor_tensor_scan(endt[:], onesf[:, 0:E], til[:], 0.0, ALU.mult, ALU.add))
            link(dve.tensor_tensor(base[:], endt[:], til[:], ALU.subtract))
            link(dve.tensor_scalar(base[:], base[:], float(P), float(P), ALU.mult, ALU.add))
            link(dve.tensor_scalar(padf[:], endt[:], float(P), iop[:, 0:1], ALU.mult, ALU.add))
            link(dve.tensor_copy(pad[:], padf[:]))
            for k in range(K2):
                kc = slice(k * C, (k + 1) * C)
                link(dve.tensor_tensor(posn[:, kc], pre[:, kc], bank[2 + k][:].rearrange("p (c e) -> p c e", e=E), ALU.subtract))
                link(dve.tensor_tensor(posn[:, kc], posn[:, kc], bank[k][:].rearrange("p (c e) -> p c e", e=E), ALU.add))
            link(dve.tensor_tensor(posn[:], posn[:], base[:].unsqueeze(1).broadcast_to([P, K2 * C, E]), ALU.add))
            link(dve.tensor_tensor(posn[:], posn[:], oh[:].rearrange("p k c e -> p (k c) e"), ALU.mult))
            link(dve.tensor_reduce(slf[:], posn[:], AX.X, ALU.add))
            link(dve.tensor_copy(slot[:], slf[:]))
            link(dve.tensor_tensor(ge[:], iot[:].unsqueeze(2).broadcast_to([P, TILES, E]),
                                   endt[:].unsqueeze(1).broadcast_to([P, TILES, E]), ALU.is_ge))
            link(dve.tensor_reduce(tef[:], ge[:], AX.X, ALU.add))
            link(dve.tensor_scalar(tef[:], tef[:], float(E - 1), None, ALU.min))
            link(dve.tensor_copy(tile_e[:], tef[:]))
            barrier(dve, 1)

            for t in (Gf, Gh, Gl):
                link(dve.memset(t[:] if t is Gf else t[:].bitcast(f32), 0.0))
            link(dve.memset(vx[:, :, :, DH:VE], 1.0))

            def transposed_lo(c, s, job_par):
                dve.wait_ge(e_xTh, ev(1, c))
                dve.tensor_tensor(xTl[:, s, :], wide(job_par, "xT")[:, 0:P], xTh[:, s, :], ALU.subtract).then_inc(e_xTl, 1)

            def u_lo(c, s, q):
                dve.wait_ge(e_uh, ev(4, c, q))
                dve.scalar_tensor_tensor(ul[:, q].rearrange("p h i -> p (h i)"), wide(s, f"u{q}")[:], 1.0 / D,
                                         uh[:, q].rearrange("p h i -> p (h i)"), ALU.add, ALU.subtract).then_inc(e_ul, 1)

            def mask(c, s, q):
                dve.wait_ge(a_s, ev(4, c, q))
                dve.wait_ge(a_num, ev(4, c - 1, q))
                dve.tensor_tensor(Am[:, q], wide(s, f"s{q}")[:].rearrange("p (h i) -> p h i", i=P),
                                  causal[:].unsqueeze(1).broadcast_to([P, HQ, P]), ALU.mult).then_inc(e_A, 1)

            def T_lo(c, s, n):
                dve.wait_ge(e_Th, ev(2, c, n))
                dve.tensor_tensor(Tl[:, s, 8 * n:8 * n + 8, 0:DH],
                                  wide(s, f"T{n}")[:].rearrange("p (h e) -> p h e", e=DH),
                                  Th[:, s, 8 * n:8 * n + 8, 0:DH], ALU.subtract).then_inc(e_Tl, 1)

            def norm(c, q):
                num = bank[4 + q % 2][:, 0:HQ * VE].rearrange("p (h e) -> p h e", e=VE)
                dve.wait_ge(a_num, ev(4, c, q))
                dve.reciprocal(rden[:, q, :], num[:, :, DH]).then_inc(e_r, 1)
                dve.wait_ge(e_r, ev(4, c, q))
                dve.wait_ge(a_nT, ev(4, c - 1, q))
                dve.tensor_tensor(nn[:, q], num[:, :, 0:DH],
                                  rden[:, q, :].unsqueeze(2).broadcast_to([P, HQ, DH]), ALU.mult).then_inc(e_nn, 1)

            def G_add(c, s):
                dve.wait_ge(a_G, ev(1, c))
                dve.wait_ge(a_T, ev(2, c, 1))
                dve.tensor_tensor(Gf[:], wide(s, "G")[:, 0:D + 2], Gf[:], ALU.add).then_inc(e_G, 1)

            transposed_lo(0, 0, 1)
            link(dve.memset(Th[:, 0, :, DH:VE].bitcast(f32), 0.0))
            link(dve.memset(Tl[:, 0, :, DH:VE].bitcast(f32), 0.0))
            dve.sem_inc(e_Gs, 1)
            dve.sem_inc(s_new, 1)

            def G_split(c, s, first):
                dve.wait_ge(e_G, ev(1, c))
                dve.wait_ge(a_num, ev(4, c - 1, 3))
                dve.tensor_copy(Gh[:], Gf[:]).then_inc(s_gh, 1)
                dve.wait_ge(s_gh, 1 + first)
                dve.tensor_tensor(Gl[:], Gf[:], Gh[:], ALU.subtract).then_inc(s_gl, 1)
                dve.tensor_copy(Th[:, 1 - s, :, DH:VE], Gf[:, D:D + 2].unsqueeze(1).broadcast_to([P, H, 2]))
                dve.wait_ge(s_gl, 1 + first)
                dve.tensor_copy(Tl[:, 1 - s, :, DH:VE], Gl[:, D:D + 2].bitcast(f32).unsqueeze(1).broadcast_to([P, H, 2])).then_inc(e_Gs, 1)

            with dve.Fori(0, B) as b:
                with dve.Fori(0, CB // 2) as p:
                    for s in range(2):
                        c = b * CB + p * 2 + s
                        u_lo(c, s, 0)
                        u_lo(c, s, 1)
                        mask(c, s, 0)
                        u_lo(c, s, 2)
                        mask(c, s, 1)
                        T_lo(c, s, 0)
                        u_lo(c, s, 3)
                        mask(c, s, 2)
                        T_lo(c, s, 1)
                        norm(c, 0)
                        mask(c, s, 3)
                        G_add(c, s)
                        transposed_lo(c + 1, 1 - s, s)
                        norm(c, 1)
                        G_split(c, s, c)
                        norm(c, 2)
                        norm(c, 3)
                        dve.wait_ge(a_y, ev(1, c))
                        dve.tensor_tensor(xa[:, bass.ds(c, 1), :].rearrange("p a d -> p (a d)"), bank[7][:, 0:D],
                                          xa[:, bass.ds(c, 1), :].rearrange("p a d -> p (a d)"), ALU.add).then_inc(e_y, 1)
                dve.wait_ge(e_Gs, (b + 1) * CB + 1)
                for t in (Gf, Gh, Gl):
                    dve.memset(t[:] if t is Gf else t[:].bitcast(f32), 0.0)
                dve.memset(Th[:, 0, :, DH:VE].bitcast(f32), 0.0)
                dve.memset(Tl[:, 0, :, DH:VE].bitcast(f32), 0.0).then_inc(s_new, 1)
                dve.wait_ge(s_new, b + 2)
            barrier(dve, 2)

            for e in range(E):
                dve.wait_ge(f_wh, 3 * (e + 1))
                dve.tensor_tensor(gul[:, e], guf[:], guh[:, e], ALU.subtract)
                dve.tensor_tensor(dnl[:, e, 0:2, :], dnf[:, 0:2, :], dnh[:, e, 0:2, :], ALU.subtract).then_inc(f_wl, 1)
                dve.tensor_tensor(dnl[0:96, e, 2, :], dnf[0:96, 2, :], dnh[0:96, e, 2, :], ALU.subtract).then_inc(f_wl, 1)
            with dve.Fori(0, TILES // 2) as i2:
                for s in range(2):
                    i = i2 * 2 + s
                    dve.wait_ge(f_xTh, ev(1, i))
                    dve.tensor_tensor(xtTl[:, s, :], bank[0][:, 0:P], xtTh[:, s, :], ALU.subtract).then_inc(f_xTl, 1)
                    dve.wait_ge(f_sl, ev(1, i))
                    dve.wait_ge(f_u, ev(1, i))
                    dve.wait_ge(f_aT, ev(1, i - 2))
                    dve.tensor_tensor(act_[:, s, :], bank[3 + s][:, 0:F], sl[:, s, :], ALU.mult).then_inc(f_act, 1)
                    dve.wait_ge(f_aTh, ev(1, i))
                    dve.tensor_tensor(aTl[:, s, 0:2, :], bank[5][:, 0:2 * P].rearrange("p (t i) -> p t i", t=2),
                                      aTh[:, s, 0:2, :], ALU.subtract)
                    dve.tensor_tensor(aTl[0:96, s, 2, :], bank[5][0:96, 2 * P:3 * P],
                                      aTh[0:96, s, 2, :], ALU.subtract).then_inc(f_aTl, 1)
            barrier(dve, 3)
            with dve.Fori(0, C // 2) as c2:
                for s in range(2):
                    c = c2 * 2 + s
                    dve.wait_ge(o_g[s], 16 * K2 * c2 + 16 * K2)
                    dve.wait_ge(o_out[s], 16 * c2 + 16)
                    dve.scalar_tensor_tensor(ot[:, s, :], gx[:, s, 0, :], wtop[:, 0, bass.ds(c, 1)],
                                             xa[:, bass.ds(c, 1), :].rearrange("p a d -> p (a d)"),
                                             ALU.mult, ALU.add).then_inc(o_h, 1)
                    dve.wait_ge(o_h, c + 1)
                    dve.scalar_tensor_tensor(ot[:, s, :], gx[:, s, 1, :], wtop[:, 1, bass.ds(c, 1)],
                                             ot[:, s, :], ALU.mult, ALU.add).then_inc(o_c, 1)

        @block.tensor
        def _(pe):
            start_ahead(pe, (n_xT, 1), (n_qk, 4), (n_lg, 1), (a_u, 4), (a_v, 2), (a_s, 4), (a_T, 2), (a_G, 1),
                        (a_xT, 1), (a_num, 4), (a_nT, 4), (a_y, 1), (f_xT, 1), (f_g, 1), (f_u, 1), (f_aT, 1), (f_y, 1))

            def split3(dst, ah, al, bh, bl, start=True, stop=True):
                pe.matmul(dst, ah, bh, start=start, stop=False)
                pe.matmul(dst, al, bh, start=False, stop=False)
                return pe.matmul(dst, ah, bl, start=False, stop=stop)

            pe.wait_ge(w_in[3], 16)
            pe.wait_ge(s_ctr, 3)
            pe.wait_ge(s_const, 1)
            natural = {"q": wqn, "k": wkn, "v": wvn, "o": won}
            los = 0
            for j, (kind, n) in enumerate(SETUP):
                if j >= 4:
                    pe.wait_ge(s_trh, j - 3)
                    if SETUP[j - 4][0] in "qkv":
                        los += 1
                        pe.wait_ge(s_trl, los)
                for i in range(4):
                    dst = bank[j % 4][:, P * i:P * i + P]
                    if kind == "M":
                        h = 8 * (n // 2) + n % 2 + 2 * i
                        r = slice(DH * (h % 2), DH * (h % 2) + DH)
                        last = pe.matmul(dst, wqn[r, h // 2, :], wkn[r, h // 2, :], start=True, stop=True)
                    else:
                        last = pe.transpose(dst, natural[kind][:, 4 * n + i, :], ident[:])
                last.then_inc(s_tr, 1)
            pe.wait_ge(s_trh, len(SETUP) + 1)
            pe.wait_ge(s_trl, 7)

            with pe.Fori(0, C // 2) as c2:
                for s in range(2):
                    c = c2 * 2 + s
                    pe.wait_ge(n_xn, ev(1, c))
                    pe.wait_ge(n_xTl, ev(1, c - 2))
                    pe.transpose(bank[4 + s][:, 0:P], xn[:, s, 0:D], ident[:]).then_inc(n_xT, 1)
                    pe.wait_ge(n_xTl, ev(1, c))
                    xh, xl = xTh[:, s, :], xTl[:, s, :]
                    for j in range(4):
                        pe.wait_ge(n_sq, ev(4, c - 1, j))
                        w = slice(512 * j, 512 * j + 512)
                        split3(bank[j][:], xh, xl, WNh[:, w], WNl[:, w]).then_inc(n_qk, 1)
                    pe.wait_ge(n_lc, ev(1, c - 2))
                    split3(bank[6 + s][:, 0:E], xh, xl, rwh[:], rwl[:]).then_inc(n_lg, 1)
            pe.wait_ge(r_oh, 2)
            pe.wait_ge(n_sq, ev(4, C - 1, 3))
            for k in range(K2):
                pe.matmul(bank[k][:], before[:], ohb[:, k].rearrange("p c e -> p (c e)"), start=True, stop=True)
                last = pe.matmul(bank[2 + k][:], ones[:], ohb[:, k].rearrange("p c e -> p (c e)"), start=True, stop=True)
            last.then_inc(r_cnt, 1)
            barrier(pe, 1)

            def transpose_x(c, s, job_par):
                pe.wait_ge(e_xn, ev(1, c))
                pe.transpose(wide(job_par, "xT")[:, 0:P], xn[:, s, 0:D], ident[:]).then_inc(a_xT, 1)

            def u(c, s, q):
                wait_wide(pe, c, f"u{q}")
                for h in range(HQ * q, HQ * q + HQ):
                    last = split3(wide(s, f"u{q}")[:, P * (h % HQ):P * (h % HQ) + P],
                                  Mh[:, h, :], Ml[:, h, :], xTh[:, s, :], xTl[:, s, :])
                last.then_inc(a_u, 1)

            def v(c, s, n):
                wait_wide(pe, c, f"v{n}")
                w = slice(512 * n, 512 * n + 512)
                split3(wide(s, f"v{n}")[:], xTh[:, s, :], xTl[:, s, :], Wvh[:, w], Wvl[:, w]).then_inc(a_v, 1)

            def scores(c, s, q):
                wait_wide(pe, c, f"s{q}")
                pe.wait_ge(e_ul, ev(4, c, q))
                split3(wide(s, f"s{q}")[:], xTh[:, s, :], xTl[:, s, :],
                       uh[:, q].rearrange("p h i -> p (h i)"), ul[:, q].rearrange("p h i -> p (h i)")).then_inc(a_s, 1)

            def T(c, s, n):
                wait_wide(pe, c, f"T{n}")
                w = slice(512 * n, 512 * n + 512)
                split3(wide(s, f"T{n}")[:], Gh[:, 0:D], Gl[:, 0:D], Wvh[:, w], Wvl[:, w]).then_inc(a_T, 1)

            def G(c, s):
                wait_wide(pe, c, "G")
                pe.matmul(wide(s, "G")[:, 0:D + 2], xn[:, s, 0:D], xn[:, s, :], start=True, stop=True).then_inc(a_G, 1)

            def num(c, s, q):
                dst = bank[4 + q % 2]
                pe.wait_ge(e_nn, ev(4, c, q - 2) if q >= 2 else ev(4, c - 1, q + 2))
                pe.wait_ge(e_v, ev(2, c, q // 2))
                pe.wait_ge(e_Tl, ev(2, c, q // 2))
                pe.wait_ge(e_A, ev(4, c, q))
                for i in range(HQ):
                    h = HQ * q + i
                    o = dst[:, VE * i:VE * i + VE]
                    pe.matmul(o, Am[:, q, i, :], vx[:, s, h, :], start=True, stop=False)
                    last = split3(o, uh[:, q, i, :], ul[:, q, i, :], Th[:, s, h, :], Tl[:, s, h, :], start=False)
                last.then_inc(a_num, 1)

            def transpose_num(c, q):
                pe.wait_ge(e_nn, ev(4, c, q))
                pe.wait_ge(e_nT, ev(4, c, q - 1) if q else ev(4, c - 1, 3))
                for t in range(2):
                    last = pe.transpose(bank[6][:, P * t:P * t + P],
                                        nn[:, q, 2 * t:2 * t + 2, :].rearrange("p h e -> p (h e)"), ident[:])
                last.then_inc(a_nT, 1)

            def y(c, q):
                if q == 0:
                    pe.wait_ge(e_y, ev(1, c - 1))
                pe.wait_ge(e_nT, ev(4, c, q))
                for t in range(2):
                    last = pe.matmul(bank[7][:, 0:D], nT[:, q, t, :], WoT[:, 2 * q + t, :],
                                     start=(q == 0 and t == 0), stop=(q == Q - 1 and t == 1))
                if q == Q - 1:
                    last.then_inc(a_y, 1)

            transpose_x(0, 0, 1)
            with pe.Fori(0, B) as b:
                for q in range(Q):
                    pe.wait_ge(e_M, 4 * b + q + 1 + 4 * AHEAD)
                pe.wait_ge(s_new, b + 1)
                pe.sem_inc(s_pass, 1)
                with pe.Fori(0, CB // 2) as p:
                    for s in range(2):
                        c = b * CB + p * 2 + s
                        pe.wait_ge(e_xTl, ev(1, c))
                        u(c, s, 0)
                        u(c, s, 1)
                        v(c, s, 0)
                        scores(c, s, 0)
                        v(c, s, 1)
                        u(c, s, 2)
                        scores(c, s, 1)
                        pe.wait_ge(e_Gs, c + 1)
                        T(c, s, 0)
                        u(c, s, 3)
                        scores(c, s, 2)
                        T(c, s, 1)
                        num(c, s, 0)
                        scores(c, s, 3)
                        G(c, s)
                        wait_wide(pe, c, "xT")
                        transpose_x(c + 1, 1 - s, s)
                        num(c, s, 1)
                        transpose_num(c, 0)
                        num(c, s, 2)
                        transpose_num(c, 1)
                        y(c, 0)
                        num(c, s, 3)
                        transpose_num(c, 2)
                        y(c, 1)
                        transpose_num(c, 3)
                        y(c, 2)
                        y(c, 3)
            barrier(pe, 2)

            pe.wait_ge(f_wl, 2 * E)
            with pe.Fori(0, TILES // 2) as i2:
                for s in range(2):
                    i = i2 * 2 + s
                    ex = pe.value_load(tile_e[0:1, bass.ds(i, 1)], min_val=0, max_val=E - 1)
                    pe.wait_ge(f_xt[s], 16 * i2 + 16)
                    pe.wait_ge(f_xTl, ev(1, i - 1))
                    pe.transpose(bank[0][:, 0:P], xt[:, s, :], ident[:]).then_inc(f_xT, 1)
                    pe.wait_ge(f_xTl, ev(1, i))
                    for g, sem_, free, b0 in ((0, f_g, f_sl, 1), (1, f_u, f_act, 3)):
                        pe.wait_ge(free, ev(1, i - 2))
                        dst = bank[b0 + s][:, 0:F]
                        pe.matmul(dst, xtTh[:, s, :], guh[:, bass.ds(ex, 1), g, :].rearrange("p a f -> p (a f)"), start=True, stop=False)
                        pe.matmul(dst, xtTl[:, s, :], guh[:, bass.ds(ex, 1), g, :].rearrange("p a f -> p (a f)"), start=False, stop=False)
                        pe.matmul(dst, xtTh[:, s, :], gul[:, bass.ds(ex, 1), g, :].rearrange("p a f -> p (a f)"), start=False, stop=True).then_inc(sem_, 1)
                    pe.wait_ge(f_act, ev(1, i))
                    pe.wait_ge(f_aTl, ev(1, i - 1))
                    for t, (o, n) in enumerate(FT):
                        last = pe.transpose(bank[5][0:n, P * t:P * t + P], act_[:, s, o:o + n], ident[:])
                    last.then_inc(f_aT, 1)
                    pe.wait_ge(f_aTl, ev(1, i))
                    pe.wait_ge(f_yt, ev(1, i - 2))
                    dst = bank[6 + s][:, 0:D]
                    for t, (o, n) in enumerate(FT):
                        wh = dnh[0:n, bass.ds(ex, 1), t, :].rearrange("p a f -> p (a f)")
                        wl = dnl[0:n, bass.ds(ex, 1), t, :].rearrange("p a f -> p (a f)")
                        last = split3(dst, aTh[0:n, s, t, :], aTl[0:n, s, t, :], wh, wl, start=(t == 0), stop=(t == 2))
                    last.then_inc(f_y, 1)
            barrier(pe, 3)


_INS = ["L0_attn_X", "L0_attn_Wq", "L0_attn_Wk", "L0_attn_Wv", "L0_attn_Wo", "L0_attn_bo",
        "L0_ffn_router_w", "L0_ffn_gate_proj", "L0_ffn_up_proj", "L0_ffn_down_proj"]


def kernel(**inputs):
    import numpy as np
    import concourse.bacc as bacc
    from concourse import mybir as mb
    from concourse.bass_utils import run_bass_kernel_spmd as run

    nc = bacc.Bacc("TRN2", target_bir_lowering=False, num_devices=1)
    arrays, args = {}, []
    for name in _INS:
        a = np.ascontiguousarray(inputs[name])
        arrays[f"in_{name}"] = a
        args.append(nc.dram_tensor(f"in_{name}", a.shape, mb.dt.from_np(a.dtype), kind="ExternalInput").ap())
    args.append(nc.dram_tensor("out_0", (C, P, D), mb.dt.float32, kind="ExternalOutput").ap())
    build(nc, *args)
    r = run(nc, [arrays], core_ids=[0])
    return r.results[0]["out_0"].reshape(B, N, D)
```

```python
import concourse.bass as bass
from concourse import mybir
from contextlib import ExitStack

B, N, D = 8, 1024, 128
H, DH = 16, 64
E, F = 8, 352
P = 128
C = B * N // P
CB = N // P
Q, HQ = 4, H // 4
U = 8
VE = DH + 2
K2 = 2
TILES = K2 * C + E
SLOTS = (TILES + 2) * P
ROW = D + 4
DST, WGT = D, D + 1
SPARE = 2 * E + 1
RT = 4
FT = 3
AHEAD = 4
EPS = 1e-5


def build(nc, x, wq, wk, wv, wo, bo, rw, gate, up, down, out):
    f32, f32r, bf16 = mybir.dt.float32, mybir.dt.float32r, mybir.dt.bfloat16
    i32, u32 = mybir.dt.int32, mybir.dt.uint32
    ALU, ACT, AX = mybir.AluOpType, mybir.ActivationFunctionType, mybir.AxisListType

    xs_d = nc.dram_tensor("sorted_tokens", (SLOTS, ROW), f32, kind="Internal").ap()
    ys_d = nc.dram_tensor("expert_rows", (K2 * B * N + SPARE * P, D), f32, kind="Internal").ap()

    ctx = ExitStack()
    with ctx:
        at = [nc.sbuf_base]

        def place(name, shape, dt=f32, size=4):
            n = size
            for d in shape[1:]:
                n *= d
            t = nc.alloc_sbuf_tensor_at(name, shape, dt, offset=at[0])
            at[0] += -(-n // 32) * 32
            return t

        at[0] = -(-at[0] // 32) * 32
        xa = place("xa", [P, C + 3, D])
        mv = place("mv", [P, C, 2])
        rstd = place("rstd", [P, C + 3])
        nmr = place("nmr", [P, C + 3])
        nmr1 = place("nmr1", [P, C + 3])
        wmean = place("wmean", [P, 3, 8])
        t64 = place("t64", [P, 2, C])
        xn = place("xn", [P, 4, D + 2])
        xTh, xTl = place("xTh", [P, 2, 2 * P], f32r), place("xTl", [P, 2, 2 * P], f32r)
        ident = place("ident", [P, P])
        causal = place("causal", [P, P])
        before = place("before", [P, P], bf16, 2)
        ones = place("ones", [P, P], bf16, 2)
        onesf = place("onesf", [P, P])
        blank = place("blank", [P, SPARE, ROW])
        bob = place("bob", [P, D])
        Mf = place("Mf", [P, H, D])
        Mh, Ml = place("Mh", [P, H, D], f32r), place("Ml", [P, H, D], f32r)
        Mt = place("Mt", [P, 2, D])
        Wvh, Wvl = place("Wvh", [P, H * DH], f32r), place("Wvl", [P, H * DH], f32r)
        WoT = place("WoT", [P, 8, D])
        cc = place("cc", [P, B, H])
        slot = place("slot", [P, C, K2], i32)
        meta = place("meta", [P, C, K2, 2])
        pad = place("pad", [P, E], i32)
        dump = place("dump", [P, 1], i32)
        tile_e = place("tile_e", [P, TILES + 1], i32)
        sidx = place("sidx", [P, 2, K2], i32)
        pay = place("pay", [P, 2, K2, ROW])
        shared = at[0]
        WNh, WNl = place("WNh", [P, 2 * H * DH], f32r), place("WNl", [P, 2 * H * DH], f32r)
        rwf = place("rwf", [P, E])
        xTf = place("xTf", [P, 2, P])
        wqn, wkn, wvn, won = (place(n, [P, 8, D]) for n in ("wqn", "wkn", "wvn", "won"))
        sq = place("sq", [P, 4, 512])
        ssq = place("ssq", [P, C, 2 * H])
        mx = place("mx", [P, B, 2 * H])
        mxa = place("mxa", [P, B, 2 * H])
        ra, rb = place("ra", [P, B, 2 * H]), place("rb", [P, B, 2 * H])
        L = place("L", [P, C, E])
        L2 = place("L2", [P, C, E])
        eqw = place("eqw", [P, C, E])
        oh = place("oh", [P, K2, C, E])
        ohb = place("ohb", [P, K2, C, E], bf16, 2)
        pre = place("pre", [P, K2 * C, E])
        posn = place("posn", [P, K2 * C, E])
        slf = place("slf", [P, K2 * C])
        m1, m2, mm = place("m1", [P, C]), place("m2", [P, C]), place("mm", [P, C])
        wtop = place("wtop", [P, K2, C])
        ord8 = place("ord8", [P, E])
        cnt, til, endt, base = (place(n, [P, E]) for n in ("cnt", "til", "endt", "base"))
        cnti = place("cnti", [P, E], i32)
        iot = place("iot", [P, TILES])
        iop = place("iop", [P, 1])
        ge = place("ge", [P, TILES, E])
        tef = place("tef", [P, TILES])
        padf = place("padf", [P, E])
        end1 = at[0]
        at[0] = shared
        uf = place("uf", [P, U, 2, 2 * P])
        uh, ul = place("uh", [P, U, 2, 2 * P], f32r), place("ul", [P, U, 2, 2 * P], f32r)
        Am = place("Am", [P, Q, HQ, P])
        vx = place("vx", [P, 2, H, VE])
        Tx = place("Tx", [P, 2, H, VE])
        Gf = place("Gf", [P, D + 2])
        Gh, Gl = place("Gh", [P, D + 2], f32r), place("Gl", [P, D + 2], f32r)
        rden = place("rden", [P, 2, Q, HQ])
        nn = place("nn", [P, 2, Q, HQ, DH])
        nT = place("nT", [P, Q, 2, P])
        end2 = at[0]
        at[0] = shared
        guf = place("guf", [P, 2, 2, F])
        guh, gul = place("guh", [P, E, 2, F], f32r), place("gul", [P, E, 2, F], f32r)
        dn = place("dn", [P, E, FT, D])
        xt = place("xt", [P, RT, ROW])
        xtTh, xtTl = place("xtTh", [P, 2, P], f32r), place("xtTl", [P, 2, P], f32r)
        wd = place("wd", [P, RT, 2])
        wdi = place("wdi", [P, RT], i32)
        sl = place("sl", [P, 2, F])
        act_ = place("act_", [P, 2, FT * P])
        aT = place("aT", [P, 2, FT, P])
        yt = place("yt", [P, RT, D])
        end3 = at[0]
        at[0] = shared
        er = place("er", [P, 2, K2, CB, D])
        ot = place("ot", [P, 2, CB, D])
        assert max(end1, end2, end3, at[0]) <= nc.sbuf_usable_end, (end1, end2, end3, at[0])

        bank = [ctx.enter_context(nc.psum_tensor(f"bank{n}", [P, 512], f32)) for n in range(8)]

        sems = {}

        def sem(name):
            sems[name] = ctx.enter_context(nc.semaphore(name))
            return sems[name]

        phase = sem("phase")
        s_pass = sem("s_pass")
        x_in, w_in, bo_in = [sem(f"x_in{n}") for n in range(8)], [sem(f"w_in{n}") for n in range(5)], sem("bo_in")
        s_ctr = sem("s_ctr")
        s_const, s_pool = sem("s_const"), sem("s_pool")
        s_tr, s_trh, s_trl = sem("s_tr"), sem("s_trh"), sem("s_trl")
        s_stat, s_chain, s_rt, s_sqrt = sem("s_stat"), sem("s_chain"), sem("s_rt"), sem("s_sqrt")
        n_xn, n_xT, n_xTh, n_xTl = sem("n_xn"), sem("n_xT"), sem("n_xTh"), sem("n_xTl")
        n_qk, n_sq, n_red, n_lg, n_lc = sem("n_qk"), sem("n_sq"), sem("n_red"), sem("n_lg"), sem("n_lc")
        s_mx, s_all = sem("s_mx"), sem("s_all")
        r_oh, r_cnt = sem("r_oh"), sem("r_cnt")
        z_tail, z_out, c_xn, c_idx = sem("z_tail"), sem("z_out"), sem("c_xn"), sem("c_idx")
        c_out = [sem("c_out0"), sem("c_out1")]
        a_u, a_v, a_s, a_T, a_G, a_xT, a_num, a_nT, a_y = (
            sem(f"a_{n}") for n in ("u", "v", "s", "T", "G", "xT", "num", "nT", "y"))
        e_uf, e_ul, e_v, e_A, e_T, e_G, e_xn, e_xTh, e_xTl, e_nn, e_nT, e_y, e_M, e_r = (
            sem(f"e_{n}") for n in
            ("uf", "ul", "v", "A", "T", "G", "xn", "xTh", "xTl", "nn", "nT", "y", "M", "r"))
        s_uh = sem("s_uh")
        s_Mt, s_Mh = sem("s_Mt"), sem("s_Mh")
        s_gh, s_gl, e_Gs, s_new = sem("s_gh"), sem("s_gl"), sem("e_Gs"), sem("s_new")
        f_w, f_wh, f_wl = [sem("f_w0"), sem("f_w1")], sem("f_wh"), sem("f_wl")
        f_dn, f_dz = sem("f_dn"), sem("f_dz")
        f_xt, f_sc = [sem(f"f_xt{n}") for n in range(RT)], [sem(f"f_sc{n}") for n in range(RT)]
        f_xT, f_xTh, f_xTl, f_wd, f_wi, f_g, f_u, f_sl, f_act, f_aT, f_aTc, f_y, f_yt = (
            sem(f"f_{n}") for n in
            ("xT", "xTh", "xTl", "wd", "wi", "g", "u", "sl", "act", "aT", "aTc", "y", "yt"))
        o_in, o_out = [sem("o_in0"), sem("o_in1")], [sem("o_out0"), sem("o_out1")]
        o_a, o_b, o_h = sem("o_a"), sem("o_b"), sem("o_h")
        f_ms = sem("f_ms")

        def ev(n, c, k=0):
            return n * (c + AHEAD) + k + 1

        def start_ahead(eng, *pairs, tail=0):
            for s, n in pairs:
                eng.sem_inc(s, n * (AHEAD - tail))

        def barrier(eng, n):
            eng.drain().then_inc(phase, 1)
            eng.wait_ge(phase, 5 * n)

        JOBS = [("u", 0, 0), ("u", 0, 1), ("u", 0, 2), ("u", 0, 3), ("v", 0, 0), ("s", 0, 0), ("u", 0, 4),
                ("s", 0, 1), ("T", 0, 0), ("u", 0, 5), ("v", 0, 1), ("s", 0, 2), ("T", 0, 1), ("u", 0, 6),
                ("u", 0, 7), ("G", 0, 0), ("s", 0, 3), ("v", 1, 0), ("s", 1, 0), ("v", 1, 1), ("s", 1, 1),
                ("T", 1, 0), ("s", 1, 2), ("T", 1, 1), ("s", 1, 3), ("G", 1, 0), ("x", 2, 0), ("x", 3, 0)]
        FREED = {"u": (e_uf, U), "v": (e_v, 2), "s": (e_A, 4), "T": (e_T, 2), "G": (e_G, 1), "x": (e_xTl, 1)}

        def wide(kind, r, k=0):
            return bank[JOBS.index((kind, r, k)) % 4]

        def wait_wide(eng, p, kind, r, k=0):
            j = JOBS.index((kind, r, k)) - 4
            kind4, r4, k4 = JOBS[j]
            s, n = FREED[kind4]
            p4 = p if j >= 0 else p - 1
            eng.wait_ge(s, ev(n, p4 if kind4 == "u" else 2 * p4 + r4, k4))

        SETUP = ([("M", n) for n in range(4)] + [("q", n) for n in range(2)] +
                 [("k", n) for n in range(2)] + [("v", n) for n in range(2)] +
                 [("o", n) for n in range(2)])

        block = ctx.enter_context(nc.Block())

        @block.sync
        def _(sp):
            for n, (t, src) in enumerate(((wqn, wq), (wkn, wk), (wvn, wv))):
                sp.dma_start(t[:], src.rearrange("(t p) d -> p t d", p=P)).then_inc(w_in[n], 16)
            for n in range(8):
                sp.dma_start(xa[:, 1 + n * CB:1 + (n + 1) * CB, :],
                             x[n].rearrange("(c p) d -> p c d", p=P)).then_inc(x_in[n], 16)
            sp.dma_start(won[:], wo.rearrange("o (t d) -> o t d", d=D)).then_inc(w_in[3], 16)
            sp.dma_start(rwf[:], rw).then_inc(w_in[4], 16)
            sp.dma_start(bob[:], bo.rearrange("(a d) -> a d", a=1).broadcast_to([P, D])).then_inc(bo_in, 16)
            sp.wait_ge(s_const, 7)
            sp.dma_start(xs_d[(K2 * C + 1) * P:SLOTS, :].rearrange("(t p) d -> p t d", p=P),
                         blank[:, E:SPARE, :]).then_inc(z_tail, 16)
            sp.wait_ge(z_tail, 16)
            sp.wait_ge(bo_in, 16)
            barrier(sp, 1)
            barrier(sp, 2)
            sp.wait_ge(f_dz, 1)
            for e in range(E):
                if e >= 2:
                    sp.wait_ge(f_wl, e - 1)
                sp.dma_start(guf[:, e % 2, 0, :], gate[e]).then_inc(f_w[e % 2], 16)
                sp.dma_start(guf[:, e % 2, 1, :], up[e]).then_inc(f_w[e % 2], 16)
                sp.dma_start(dn[:, e, 0:2, :], down[e, 0:256, :].rearrange("(t p) d -> p t d", p=P)).then_inc(f_dn, 16)
                sp.dma_start(dn[0:F - 256, e, 2, :], down[e, 256:F, :]).then_inc(f_dn, 16)

            def load_tile(i, r):
                sp.dma_start(xt[:, r, :], xs_d[bass.ds((i + 1) * P, P), :]).then_inc(f_xt[r], 16)

            load_tile(0, 0)
            with sp.Fori(0, TILES // RT) as i4:
                for r in range(RT):
                    i = i4 * RT + r
                    sp.wait_ge(f_xT, ev(1, i - 3))
                    sp.wait_ge(f_wd, ev(1, i - 3))
                    load_tile(i + 1, (r + 1) % RT)
            barrier(sp, 3)
            with sp.Fori(0, B // 2) as b2:
                for s in range(2):
                    b = b2 * 2 + s
                    sp.wait_ge(o_b, ev(1, b - 2))
                    for k in range(K2):
                        sp.dma_start(er[:, s, k], ys_d[bass.ds((b + B * k) * N, N), :].rearrange("(c p) d -> p c d", p=P)
                                     ).then_inc(o_in[s], 16)
            for s in range(2):
                sp.wait_ge(o_out[s], 16 * (B // 2 + 1))

        @block.gpsimd
        def _(pool):
            start_ahead(pool, (e_M, U), (o_a, 1), (f_wi, 1))
            for t in o_out:
                pool.sem_inc(t, 16)
            pool.memset(blank[:], 0.0).then_inc(s_pool, 1)
            pool.memset(ident[:], 0.0).then_inc(s_pool, 1)
            pool.memset(causal[:], 1.0).then_inc(s_pool, 1)
            pool.memset(onesf[:], 1.0).then_inc(s_pool, 1)
            pool.memset(before[:], 1.0).then_inc(s_pool, 1)
            pool.memset(ones[:], 1.0).then_inc(s_pool, 1)
            pool.memset(xn[:, :, D:D + 2], 1.0).then_inc(s_pool, 1)
            for t in (xa[:, 0, :], xa[:, C + 1:C + 3, :], rstd[:, C + 1:C + 3], nmr[:, C + 1:C + 3], nmr1[:, C + 1:C + 3],
                      pay[:, :, :, D + 2:ROW]):
                pool.memset(t, 0.0).then_inc(s_pool, 1)
            pool.wait_ge(s_pool, 13)
            pool.affine_select(out=ident[:], in_=ident[:], compare_op=ALU.not_equal, fill=1.0,
                               base=0, pattern=[[-1, P]], channel_multiplier=1).then_inc(s_const, 1)
            pool.affine_select(out=causal[:], in_=causal[:], compare_op=ALU.is_ge, fill=0.0,
                               base=0, pattern=[[1, P]], channel_multiplier=-1).then_inc(s_const, 1)
            pool.affine_select(out=before[:], in_=before[:], compare_op=ALU.is_gt, fill=0.0,
                               base=0, pattern=[[1, P]], channel_multiplier=-1).then_inc(s_const, 1)
            pool.iota(ord8[:], pattern=[[-1, E]], base=E, channel_multiplier=0,
                      allow_small_or_imprecise_dtypes=True).then_inc(s_const, 1)
            pool.iota(iot[:], pattern=[[1, TILES]], base=0, channel_multiplier=0,
                      allow_small_or_imprecise_dtypes=True).then_inc(s_const, 1)
            pool.iota(iop[:], pattern=[[0, 1]], base=0, channel_multiplier=1,
                      allow_small_or_imprecise_dtypes=True).then_inc(s_const, 1)
            pool.iota(blank[:, :, DST], pattern=[[P, SPARE]], base=K2 * B * N, channel_multiplier=1,
                      allow_small_or_imprecise_dtypes=True).then_inc(s_const, 1)
            pool.iota(dump[:], pattern=[[0, 1]], base=K2 * B * N, channel_multiplier=1).then_inc(s_const, 1)
            pool.iota(meta[:, :, :, 0], pattern=[[P, C], [B * N, K2]], base=0, channel_multiplier=1,
                      allow_small_or_imprecise_dtypes=True).then_inc(s_const, 1)
            pool.wait_ge(s_mx, 1)
            pool.partition_all_reduce(mxa[:].rearrange("p b h -> p (b h)"), mx[:].rearrange("p b h -> p (b h)"),
                                      P, bass.bass_isa.ReduceOp.max).then_inc(s_all, 1)
            barrier(pool, 1)

            def scale_M(b):
                for g in range(U):
                    hs = slice(2 * g, 2 * g + 2)
                    pool.tensor_tensor(Mt[:], Mf[:, hs, :],
                                       cc[:, bass.ds(b, 1), hs].rearrange("p a h -> p (a h)").unsqueeze(2).broadcast_to([P, 2, D]),
                                       ALU.mult).then_inc(s_Mt, 1)
                    pool.wait_ge(s_Mt, U * b + g + 1)
                    pool.wait_ge(a_u, ev(U, 4 * b - 1, g))
                    pool.sem_inc(s_pass, 1)
                    pool.tensor_copy(Mh[:, hs, :], Mt[:]).then_inc(s_Mh, 1)
                    pool.wait_ge(s_Mh, U * b + g + 1)
                    pool.tensor_tensor(Ml[:, hs, :], Mt[:], Mh[:, hs, :], ALU.subtract).then_inc(e_M, 1)
                    pool.wait_ge(e_M, ev(U, b, g))

            def scatter(c, s, before_):
                if before_ is not None:
                    pool.wait_ge(c_out[s], 16 * K2 * before_)
                    pool.sem_inc(s_pass, 1)
                pool.tensor_copy(sidx[:, s, :], slot[:, bass.ds(c, 1), :].rearrange("p a k -> p (a k)")).then_inc(c_idx, 1)
                pool.tensor_copy(pay[:, s, :, D:D + 2], meta[:, bass.ds(c, 1)].rearrange("p a k m -> p (a k) m")).then_inc(c_idx, 1)
                pool.wait_ge(c_idx, 2 * c + 2)
                pool.wait_ge(c_xn, c + 1)
                pool.sem_inc(s_pass, 1)
                for k in range(K2):
                    pool.indirect_dma_start(
                        xs_d, bass.IndirectOffsetOnAxis(ap=sidx[:, s, k:k + 1], axis=0),
                        pay[:, s, k, :], None).then_inc(c_out[s], 16)

            scale_M(0)
            for e in range(E):
                pool.indirect_dma_start(xs_d, bass.IndirectOffsetOnAxis(ap=pad[:, e:e + 1], axis=0),
                                        blank[:, e, :], None).then_inc(z_out, 16)
            pool.wait_ge(z_out, 16 * E)
            for s in range(2):
                scatter(s, s, None)
            with pool.Fori(1, C // 4) as c2:
                for s in range(2):
                    scatter(c2 * 2 + s, s, c2)
            scale_M(1)
            with pool.Fori(C // 4, C // 2) as c2:
                for s in range(2):
                    scatter(c2 * 2 + s, s, c2)
            for s in range(2):
                pool.wait_ge(c_out[s], 16 * K2 * (C // 2))
            with pool.Fori(2, B) as b:
                scale_M(b)
            for n in range(2):
                for r in range(RT):
                    pool.indirect_dma_start(ys_d, bass.IndirectOffsetOnAxis(ap=dump[:], axis=0),
                                            blank[:, 0, 0:D], None).then_inc(f_sc[r], 16)
                    pool.wait_ge(f_sc[r], 16 * (n + 1))
            barrier(pool, 2)

            pool.memset(dn[64:P, :, FT - 1, :], 0.0).then_inc(f_dz, 1)
            with pool.Fori(0, TILES // RT) as i4:
                for r in range(RT):
                    i = i4 * RT + r
                    pool.wait_ge(f_sc[r], 16 * (i4 + 2))
                    pool.wait_ge(f_wd, ev(1, i))
                    pool.sem_inc(s_pass, 1)
                    pool.tensor_copy(wdi[:, r:r + 1], wd[:, r, 0:1]).then_inc(f_wi, 1)
                    pool.wait_ge(f_wi, ev(1, i))
                    pool.wait_ge(f_yt, ev(1, i))
                    pool.sem_inc(s_pass, 1)
                    pool.indirect_dma_start(ys_d, bass.IndirectOffsetOnAxis(ap=wdi[:, r:r + 1], axis=0),
                                            yt[:, r, :], None).then_inc(f_sc[r], 16)
            for r in range(RT):
                pool.wait_ge(f_sc[r], 16 * (TILES // RT + 2))
            barrier(pool, 3)
            with pool.Fori(0, B // 2) as b2:
                for s in range(2):
                    b = b2 * 2 + s
                    pool.wait_ge(o_in[s], 16 * K2 * (b2 + 1))
                    pool.tensor_tensor(er[:, s, 0], er[:, s, 0], bob[:].unsqueeze(1).broadcast_to([P, CB, D]), ALU.add).then_inc(o_a, 1)

        @block.scalar
        def _(act):
            start_ahead(act, (n_xn, 1), (n_xTh, 1), (n_sq, 4), (e_uf, U), (e_v, 2), (e_T, 2),
                        (e_xn, 1), (e_xTh, 1), (f_xTh, 1), (f_sl, 1))
            start_ahead(act, (e_nT, 4), (f_yt, 1), tail=1)
            place_of = {"q": (WNh, 0), "k": (WNh, 1024), "v": (Wvh, 0)}
            for j, (kind, n) in enumerate(SETUP):
                act.wait_ge(s_tr, j + 1)
                b_ = bank[j % 4]
                if kind == "M":
                    h0 = 8 * (n // 2) + n % 2
                    dst = Mf[:, h0:h0 + 7:2, :]
                    src = b_[:].rearrange("p (h d) -> p h d", d=D)
                elif kind == "o":
                    dst = WoT[:, 4 * n:4 * n + 4, :]
                    src = b_[:].rearrange("p (h d) -> p h d", d=D)
                else:
                    t, o = place_of[kind]
                    dst, src = t[:, o + 512 * n:o + 512 * n + 512], b_[:]
                act.activation(dst, src, ACT.Copy).then_inc(s_trh, 1)
            act.wait_ge(s_stat, 1)
            act.activation(t64[:, 1, :], t64[:, 0, :], ACT.Sqrt).then_inc(s_sqrt, 1)
            act.wait_ge(s_stat, 2)
            act.wait_ge(s_pool, 13)

            def normalised(dst, c, shift):
                return act.activation(dst, xa[:, bass.ds(c + 1, 1), :].rearrange("p a d -> p (a d)"), ACT.Identity,
                                      scale=rstd[:, bass.ds(c + 1, 1)], bias=shift[:, bass.ds(c + 1, 1)])

            def xn_norms(c, s):
                act.wait_ge(n_xT, ev(1, c - 2))
                normalised(xn[:, s, 0:D], c, nmr).then_inc(n_xn, 1)

            def xT_norms(c, s):
                act.wait_ge(n_xT, ev(1, c))
                act.wait_ge(n_lg, ev(1, c - 2))
                act.activation(xTh[:, s, 0:P], bank[4 + s][:, 0:P], ACT.Copy)
                act.activation(xTf[:, s, :], bank[4 + s][:, 0:P], ACT.Copy).then_inc(n_xTh, 1)

            xn_norms(0, 0)
            xT_norms(0, 0)
            with act.Fori(0, C // 2) as c2:
                for s in range(2):
                    c = c2 * 2 + s
                    xn_norms(c + 1, 1 - s)
                    for j in range(4):
                        act.wait_ge(n_qk, ev(4, c, j))
                        act.wait_ge(n_red, ev(4, c - 1, j))
                        act.activation(sq[:, j, :], bank[j][:], ACT.Square).then_inc(n_sq, 1)
                        if j == 1:
                            xT_norms(c + 1, 1 - s)
            act.wait_ge(s_all, 1)
            act.activation(ra[:], mxa[:], ACT.Sqrt).then_inc(s_sqrt, 1)
            act.wait_ge(s_rt, 1)
            act.activation(mm[:], mm[:], ACT.Exp).then_inc(s_sqrt, 1)
            barrier(act, 1)

            def for_scatter(c, s, before_):
                if before_ is not None:
                    act.wait_ge(c_out[s], 16 * K2 * before_)
                normalised(pay[:, s, 0, 0:D], c, nmr)
                normalised(pay[:, s, 1, 0:D], c, nmr).then_inc(c_xn, 1)

            def normalise(c, r):
                act.wait_ge(a_G, ev(1, c - 4))
                normalised(xn[:, r % 4, 0:D], c, nmr1).then_inc(e_xn, 1)

            def transposed(c, r):
                act.wait_ge(a_xT, ev(1, c))
                act.activation(xTh[:, r // 2 % 2, P * (r % 2):P * (r % 2) + P], wide("x", 2 + r % 2)[:, 0:P],
                               ACT.Copy).then_inc(e_xTh, 1)

            def u_out(p, g):
                act.wait_ge(a_u, ev(U, p, g))
                act.wait_ge(a_num, ev(4, 2 * p - 1, g // 2))
                act.activation(uf[:, g].rearrange("p h i -> p (h i)"), wide("u", 0, g)[:], ACT.Identity,
                               bias=1.0 / D).then_inc(e_uf, 1)

            def v_out(c, s, n):
                act.wait_ge(a_v, ev(2, c, n))
                act.wait_ge(a_num, ev(4, c - 2, 3))
                act.activation(vx[:, s, 8 * n:8 * n + 8, 0:DH],
                               wide("v", s, n)[:].rearrange("p (h e) -> p h e", e=DH), ACT.Copy).then_inc(e_v, 1)

            def T_out(c, s, n):
                act.wait_ge(a_T, ev(2, c, n))
                act.wait_ge(a_num, ev(4, c - 2, 3))
                act.activation(Tx[:, s, 8 * n:8 * n + 8, 0:DH],
                               wide("T", s, n)[:].rearrange("p (h e) -> p h e", e=DH), ACT.Copy).then_inc(e_T, 1)

            def nT_out(c, q):
                act.wait_ge(a_nT, ev(4, c, q))
                act.wait_ge(a_y, ev(1, c - 1))
                act.activation(nT[:, q].rearrange("p t i -> p (t i)"), bank[6][:, 0:2 * P], ACT.Copy).then_inc(e_nT, 1)

            def attend_pair(p, pr, sc=None, sc_half=None):
                A, Z = 2 * p, 2 * p - 1

                def slot_(m):
                    if sc is not None:
                        for_scatter(sc + m, m % 2, None if (type(sc) is int and sc + m < 2) else sc_half + m // 2)

                u_out(p, 0)
                u_out(p, 1)
                nT_out(Z, 0)
                u_out(p, 2)
                slot_(0)
                u_out(p, 3)
                nT_out(Z, 1)
                v_out(A, 0, 0)
                u_out(p, 4)
                slot_(1)
                nT_out(Z, 2)
                T_out(A, 0, 0)
                u_out(p, 5)
                v_out(A, 0, 1)
                slot_(2)
                nT_out(Z, 3)
                T_out(A, 0, 1)
                u_out(p, 6)
                u_out(p, 7)
                slot_(3)
                normalise(A + 2, 2 * pr + 2)
                normalise(A + 3, 2 * pr + 3)
                v_out(A + 1, 1, 0)
                v_out(A + 1, 1, 1)
                slot_(4)
                T_out(A + 1, 1, 0)
                nT_out(A, 0)
                T_out(A + 1, 1, 1)
                nT_out(A, 1)
                slot_(5)
                nT_out(A, 2)
                transposed(A + 2, 2 * pr + 2)
                nT_out(A, 3)
                transposed(A + 3, 2 * pr + 3)
                slot_(6)
                slot_(7)

            normalise(0, 0)
            normalise(1, 1)
            transposed(0, 0)
            transposed(1, 1)
            for pr in range(2):
                attend_pair(pr, pr, pr * 8, pr * 4)
            with act.Fori(1, 4) as c4:
                for pr in range(2):
                    attend_pair(c4 * 2 + pr, pr, (c4 * 2 + pr) * 8, (c4 * 2 + pr) * 4)
            with act.Fori(4, C // 4) as c4:
                for pr in range(2):
                    attend_pair(c4 * 2 + pr, pr)
            for q in range(Q):
                nT_out(C - 1, q)
            barrier(act, 2)

            for e in range(E):
                act.wait_ge(f_w[e % 2], 32 * (e // 2 + 1))
                act.activation(guh[:, e], guf[:, e % 2], ACT.Copy).then_inc(f_wh, 1)

            def tile_hi(i, s):
                act.wait_ge(f_xT, ev(1, i))
                act.wait_ge(f_u, ev(1, i - 2))
                act.activation(xtTh[:, s, :], bank[0][:, 0:P], ACT.Copy).then_inc(f_xTh, 1)

            def result(i, r, s, uses):
                act.wait_ge(f_y, ev(1, i))
                act.wait_ge(f_sc[r], 16 * uses)
                act.activation(yt[:, r, :], bank[6 + s][:, 0:D], ACT.Copy, scale=wd[:, r, 1:2]).then_inc(f_yt, 1)

            act.preload_act_table(ACT.Silu)
            tile_hi(0, 0)
            with act.Fori(0, TILES // RT) as i4:
                for r in range(RT):
                    i, s = i4 * RT + r, r % 2
                    act.wait_ge(f_g, ev(1, i))
                    act.wait_ge(f_act, ev(1, i - 2))
                    act.activation(sl[:, s, :], bank[1 + s][:, 0:F], ACT.Silu).then_inc(f_sl, 1)
                    tile_hi(i + 1, 1 - s)
                    result(i - 1, (r - 1) % RT, 1 - s, i4 + 2 if r else i4 + 1)
            result(TILES - 1, RT - 1, 1, TILES // RT + 1)
            barrier(act, 3)
            with act.Fori(0, B // 2) as b2:
                for s in range(2):
                    b = b2 * 2 + s
                    act.wait_ge(o_b, ev(1, b))
                    act.dma_start(out[bass.ds(b * CB, CB)].rearrange("c p d -> p c d"), ot[:, s]).then_inc(o_out[s], 16)

        @block.vector
        def _(dve):
            start_ahead(dve, (n_xTl, 1), (n_red, 4), (n_lc, 1), (e_ul, U), (e_A, 4), (e_G, 1),
                        (e_xTl, 1), (e_nn, 4), (e_r, 4), (f_xTl, 1), (f_wd, 1), (f_act, 1), (o_b, 1))
            start_ahead(dve, (e_y, 1), (f_aTc, 1), tail=1)
            links = [0]

            def link(ins):
                links[0] += 1
                ins.then_inc(s_chain, 1)
                dve.wait_ge(s_chain, links[0])

            def rsqrt(dst, val, root, tmp):
                link(dve.reciprocal(dst, root))
                link(dve.tensor_tensor(tmp, dst, dst, ALU.mult))
                link(dve.tensor_tensor(tmp, tmp, val, ALU.mult))
                link(dve.tensor_scalar(tmp, tmp, -0.5, 1.5, ALU.mult, ALU.add))
                link(dve.tensor_tensor(dst, dst, tmp, ALU.mult))

            for n, t in enumerate((wqn, wkn, wvn)):
                dve.wait_ge(w_in[n], 16)
                link(dve.tensor_reduce(wmean[:, n, :], t[:], AX.X, ALU.add))
                link(dve.tensor_scalar(wmean[:, n, :], wmean[:, n, :], 1.0 / D, None, ALU.mult))
                dve.tensor_tensor(t[:], t[:], wmean[:, n, :].unsqueeze(2).broadcast_to([P, 8, D]),
                                  ALU.subtract).then_inc(s_ctr, 1)
            for n in range(B):
                dve.wait_ge(x_in[n], 16)
                for c in range(n * CB, n * CB + CB):
                    link(dve.bn_stats(eqw[:, c, 0:6], xa[:, c + 1, :]))
                    link(dve.bn_aggr(mv[:, c, :], eqw[:, c, 0:6]))
            dve.tensor_scalar(t64[:, 0, :], mv[:, :, 1], EPS, None, ALU.add).then_inc(s_stat, 1)
            place_of = {"q": (WNl, WNh, 0), "k": (WNl, WNh, 1024), "v": (Wvl, Wvh, 0)}
            for j, (kind, n) in enumerate(SETUP):
                if kind in place_of:
                    lo, hi, o = place_of[kind]
                    dve.wait_ge(s_trh, j + 1)
                    dve.tensor_tensor(lo[:, o + 512 * n:o + 512 * n + 512], bank[j % 4][:],
                                      hi[:, o + 512 * n:o + 512 * n + 512], ALU.subtract).then_inc(s_trl, 1)
            dve.wait_ge(s_sqrt, 1)
            rsqrt(rstd[:, 1:C + 1], t64[:, 0, :], t64[:, 1, :], mm[:])
            dve.scalar_tensor_tensor(nmr[:, 1:C + 1], mv[:, :, 0], -1.0, rstd[:, 1:C + 1], ALU.mult, ALU.mult).then_inc(s_stat, 1)
            dve.wait_ge(s_stat, 2)
            dve.tensor_scalar(nmr1[:, 1:C + 1], nmr[:, 1:C + 1], 1.0, None, ALU.add).then_inc(s_stat, 1)

            def xTl_norms(c, s):
                dve.wait_ge(n_xTh, ev(1, c))
                dve.tensor_tensor(xTl[:, s, 0:P], bank[4 + s][:, 0:P], xTh[:, s, 0:P], ALU.subtract).then_inc(n_xTl, 1)

            xTl_norms(0, 0)
            with dve.Fori(0, C // 2) as c2:
                for s in range(2):
                    c = c2 * 2 + s
                    for j in range(4):
                        dve.wait_ge(n_sq, ev(4, c, j))
                        dve.tensor_reduce(ssq[:, bass.ds(c, 1), 8 * j:8 * j + 8].rearrange("p a h -> p (a h)"),
                                          sq[:, j, :].rearrange("p (h e) -> p h e", e=DH),
                                          AX.X, ALU.add).then_inc(n_red, 1)
                        if j == 1:
                            xTl_norms(c + 1, 1 - s)
                    dve.wait_ge(n_lg, ev(1, c))
                    dve.tensor_copy(L[:, bass.ds(c, 1), :].rearrange("p a e -> p (a e)"), bank[6 + s][:, 0:E]).then_inc(n_lc, 1)
            dve.wait_ge(n_red, ev(4, C - 1, 3))
            dve.wait_ge(n_lc, ev(1, C - 1))
            dve.tensor_reduce(mx[:], ssq[:].rearrange("p (b c) h -> p b h c", b=B), AX.X, ALU.max).then_inc(s_mx, 1)

            bc = [P, C, E]
            link(dve.tensor_reduce(m1[:], L[:], AX.X, ALU.max))

            def first_of(best, src, k):
                link(dve.tensor_tensor(eqw[:], src[:], best[:].unsqueeze(2).broadcast_to(bc), ALU.is_equal))
                link(dve.tensor_tensor(eqw[:], eqw[:], ord8[:].unsqueeze(1).broadcast_to(bc), ALU.mult))
                link(dve.tensor_reduce(slf[:, 0:C], eqw[:], AX.X, ALU.max))
                link(dve.tensor_tensor(oh[:, k], ord8[:].unsqueeze(1).broadcast_to(bc),
                                       slf[:, 0:C].unsqueeze(2).broadcast_to(bc), ALU.is_equal))
                dve.tensor_copy(ohb[:, k], oh[:, k]).then_inc(r_oh, 1)

            dve.wait_ge(s_const, 9)
            first_of(m1, L, 0)
            link(dve.scalar_tensor_tensor(L2[:].rearrange("p c e -> p (c e)"),
                                          oh[:, 0].rearrange("p c e -> p (c e)"), -3.0e38,
                                          L[:].rearrange("p c e -> p (c e)"), ALU.mult, ALU.add))
            link(dve.tensor_reduce(m2[:], L2[:], AX.X, ALU.max))
            first_of(m2, L2, 1)
            dve.tensor_tensor(mm[:], m2[:], m1[:], ALU.subtract).then_inc(s_rt, 1)
            dve.wait_ge(s_sqrt, 3)
            link(dve.tensor_scalar(m1[:], mm[:], 1.0, None, ALU.add))
            link(dve.reciprocal(wtop[:, 0, :], m1[:]))
            link(dve.tensor_tensor(wtop[:, 1, :], wtop[:, 0, :], mm[:], ALU.mult))
            link(dve.tensor_copy(meta[:, :, :, 1], wtop[:].rearrange("p k c -> p c k")))
            rsqrt(rb[:], mxa[:], ra[:], mx[:])
            link(dve.tensor_tensor(cc[:], rb[:, :, 0:H], rb[:, :, H:2 * H], ALU.mult))
            dve.wait_ge(r_cnt, 1)
            for k in range(K2):
                for e in range(E):
                    first = 0.0 if k == 0 else pre[:, C - 1, e:e + 1]
                    link(dve.tensor_tensor_scan(pre[:, k * C:(k + 1) * C, e], onesf[:, 0:C],
                                                bank[2 + k][:].rearrange("p (c e) -> p c e", e=E)[:, :, e],
                                                first, ALU.mult, ALU.add))
            link(dve.tensor_copy(cnt[:], pre[:, K2 * C - 1, :]))
            link(dve.tensor_scalar(til[:], cnt[:], float(P - 1), None, ALU.add))
            link(dve.tensor_copy(cnti[:], til[:]))
            link(dve.tensor_single_scalar(cnti[:], cnti[:], 7, ALU.logical_shift_right))
            link(dve.tensor_copy(til[:], cnti[:]))
            link(dve.tensor_tensor_scan(endt[:], onesf[:, 0:E], til[:], 0.0, ALU.mult, ALU.add))
            link(dve.tensor_tensor(base[:], endt[:], til[:], ALU.subtract))
            link(dve.tensor_scalar(base[:], base[:], float(P), float(P), ALU.mult, ALU.add))
            link(dve.tensor_scalar(padf[:], endt[:], float(P), iop[:, 0:1], ALU.mult, ALU.add))
            link(dve.tensor_copy(pad[:], padf[:]))
            for k in range(K2):
                kc = slice(k * C, (k + 1) * C)
                link(dve.tensor_tensor(posn[:, kc], pre[:, kc], bank[2 + k][:].rearrange("p (c e) -> p c e", e=E), ALU.subtract))
                link(dve.tensor_tensor(posn[:, kc], posn[:, kc], bank[k][:].rearrange("p (c e) -> p c e", e=E), ALU.add))
            link(dve.tensor_tensor(posn[:], posn[:], base[:].unsqueeze(1).broadcast_to([P, K2 * C, E]), ALU.add))
            link(dve.tensor_tensor(posn[:], posn[:], oh[:].rearrange("p k c e -> p (k c) e"), ALU.mult))
            link(dve.tensor_reduce(slf[:], posn[:], AX.X, ALU.add))
            link(dve.tensor_copy(slot[:].rearrange("p c k -> p k c"), slf[:].rearrange("p (k c) -> p k c", k=K2)))
            link(dve.tensor_tensor(ge[:], iot[:].unsqueeze(2).broadcast_to([P, TILES, E]),
                                   endt[:].unsqueeze(1).broadcast_to([P, TILES, E]), ALU.is_ge))
            link(dve.tensor_reduce(tef[:], ge[:], AX.X, ALU.add))
            link(dve.tensor_scalar(tef[:], tef[:], float(E - 1), None, ALU.min))
            link(dve.memset(tile_e[:, 0:1], 0))
            link(dve.tensor_copy(tile_e[:, 1:TILES + 1], tef[:]))
            barrier(dve, 1)

            for t in (Gf, Gh, Gl):
                link(dve.memset(t[:] if t is Gf else t[:].bitcast(f32), 0.0))
            link(dve.memset(vx[:, :, :, DH:VE], 1.0))
            link(dve.memset(Tx[:, 0, :, DH:VE], 0.0))
            link(dve.memset(nn[:], 0.0))
            dve.sem_inc(e_Gs, 1)
            dve.sem_inc(s_new, 1)

            def transposed_lo(c, r):
                t = slice(P * (r % 2), P * (r % 2) + P)
                dve.wait_ge(e_xTh, ev(1, c))
                dve.tensor_tensor(xTl[:, r // 2 % 2, t], wide("x", 2 + r % 2)[:, 0:P],
                                  xTh[:, r // 2 % 2, t], ALU.subtract).then_inc(e_xTl, 1)

            def u_split(p, g):
                dve.wait_ge(e_uf, ev(U, p, g))
                dve.tensor_copy(uh[:, g], uf[:, g]).then_inc(s_uh, 1)
                dve.wait_ge(s_uh, U * p + g + 1)
                dve.tensor_tensor(ul[:, g], uf[:, g], uh[:, g], ALU.subtract).then_inc(e_ul, 1)

            def mask(c, s, q):
                dve.wait_ge(a_s, ev(4, c, q))
                dve.wait_ge(a_num, ev(4, c - 1, q))
                dve.tensor_tensor(Am[:, q], wide("s", s, q)[:].rearrange("p (h i) -> p h i", i=P),
                                  causal[:].unsqueeze(1).broadcast_to([P, HQ, P]), ALU.mult).then_inc(e_A, 1)

            def norm(c, s, q):
                num = bank[4 + q % 2][:, 0:HQ * VE].rearrange("p (h e) -> p h e", e=VE)
                dve.wait_ge(a_num, ev(4, c, q))
                dve.reciprocal(rden[:, s, q, :], num[:, :, DH]).then_inc(e_r, 1)
                dve.wait_ge(e_r, ev(4, c, q))
                dve.wait_ge(a_nT, ev(4, c - 2, q))
                dve.tensor_tensor(nn[:, s, q], num[:, :, 0:DH],
                                  rden[:, s, q, :].unsqueeze(2).broadcast_to([P, HQ, DH]), ALU.mult).then_inc(e_nn, 1)

            def G_add(c, s):
                dve.wait_ge(a_G, ev(1, c))
                dve.tensor_tensor(Gf[:], wide("G", s)[:, 0:D + 2], Gf[:], ALU.add).then_inc(e_G, 1)

            def G_split(c, s):
                dve.wait_ge(e_G, ev(1, c))
                dve.wait_ge(a_T, ev(2, c, 1))
                dve.wait_ge(a_num, ev(4, c - 1, 3))
                dve.tensor_copy(Gh[:], Gf[:]).then_inc(s_gh, 1)
                dve.tensor_copy(Tx[:, 1 - s, :, DH:VE], Gf[:, D:D + 2].unsqueeze(1).broadcast_to([P, H, 2]))
                dve.wait_ge(s_gh, c + 1)
                dve.tensor_tensor(Gl[:], Gf[:], Gh[:], ALU.subtract).then_inc(e_Gs, 1)

            def y_add(c):
                dve.wait_ge(a_y, ev(1, c))
                dve.tensor_tensor(xa[:, bass.ds(c + 1, 1), :].rearrange("p a d -> p (a d)"), bank[7][:, 0:D],
                                  xa[:, bass.ds(c + 1, 1), :].rearrange("p a d -> p (a d)"), ALU.add).then_inc(e_y, 1)

            transposed_lo(0, 0)
            transposed_lo(1, 1)
            with dve.Fori(0, B) as b:
                with dve.Fori(0, CB // 4) as half:
                    for pr in range(2):
                        p = b * (CB // 2) + half * 2 + pr
                        A = 2 * p
                        u_split(p, 0)
                        u_split(p, 1)
                        u_split(p, 2)
                        u_split(p, 3)
                        mask(A, 0, 0)
                        u_split(p, 4)
                        mask(A, 0, 1)
                        u_split(p, 5)
                        norm(A, 0, 0)
                        mask(A, 0, 2)
                        norm(A, 0, 1)
                        u_split(p, 6)
                        u_split(p, 7)
                        G_add(A, 0)
                        norm(A, 0, 2)
                        y_add(A - 1)
                        mask(A, 0, 3)
                        G_split(A, 0)
                        mask(A + 1, 1, 0)
                        norm(A, 0, 3)
                        mask(A + 1, 1, 1)
                        norm(A + 1, 1, 0)
                        mask(A + 1, 1, 2)
                        norm(A + 1, 1, 1)
                        mask(A + 1, 1, 3)
                        norm(A + 1, 1, 2)
                        G_add(A + 1, 1)
                        G_split(A + 1, 1)
                        transposed_lo(A + 2, 2 * pr + 2)
                        transposed_lo(A + 3, 2 * pr + 3)
                        y_add(A)
                        norm(A + 1, 1, 3)
                dve.wait_ge(e_Gs, (b + 1) * CB + 1)
                for t in (Gf, Gh, Gl):
                    dve.memset(t[:] if t is Gf else t[:].bitcast(f32), 0.0)
                dve.memset(Tx[:, 0, :, DH:VE], 0.0).then_inc(s_new, 1)
                dve.wait_ge(s_new, b + 2)
            y_add(C - 1)
            barrier(dve, 2)

            dve.memset(act_[:], 0.0).then_inc(f_ms, 1)
            dve.memset(wd[:], 0.0).then_inc(f_ms, 1)
            for e in range(E):
                dve.wait_ge(f_wh, e + 1)
                dve.tensor_tensor(gul[:, e], guf[:, e % 2], guh[:, e], ALU.subtract).then_inc(f_wl, 1)

            def tile_lo(i, s):
                dve.wait_ge(f_xTh, ev(1, i))
                dve.tensor_tensor(xtTl[:, s, :], bank[0][:, 0:P], xtTh[:, s, :], ALU.subtract).then_inc(f_xTl, 1)

            def tile_meta(i, r):
                dve.wait_ge(f_wi, ev(1, i - RT))
                dve.wait_ge(f_yt, ev(1, i - RT))
                dve.tensor_copy(wd[:, r, :], xt[:, r, D:D + 2]).then_inc(f_wd, 1)

            def hidden_out(i, s):
                dve.wait_ge(f_aT, ev(1, i))
                dve.wait_ge(f_y, ev(1, i - 2))
                dve.tensor_copy(aT[:, s].rearrange("p t i -> p (t i)"), bank[5][:, 0:FT * P]).then_inc(f_aTc, 1)

            dve.wait_ge(f_ms, 2)
            tile_lo(0, 0)
            tile_meta(0, 0)
            with dve.Fori(0, TILES // RT) as i4:
                for r in range(RT):
                    i, s = i4 * RT + r, r % 2
                    hidden_out(i - 1, 1 - s)
                    dve.wait_ge(f_sl, ev(1, i))
                    dve.wait_ge(f_u, ev(1, i))
                    dve.wait_ge(f_aT, ev(1, i - 2))
                    dve.tensor_tensor(act_[:, s, 0:F], bank[3 + s][:, 0:F], sl[:, s, :], ALU.mult).then_inc(f_act, 1)
                    tile_lo(i + 1, 1 - s)
                    tile_meta(i + 1, (r + 1) % RT)
            hidden_out(TILES - 1, 1)
            barrier(dve, 3)
            with dve.Fori(0, B // 2) as b2:
                for s in range(2):
                    b = b2 * 2 + s
                    dve.wait_ge(o_in[s], 16 * K2 * (b2 + 1))
                    dve.wait_ge(o_out[s], 16 * (b2 + 1))
                    dve.tensor_tensor(ot[:, s], er[:, s, 1], xa[:, bass.ds(b * CB + 1, CB), :], ALU.add).then_inc(o_h, 1)
                    dve.wait_ge(o_h, b + 1)
                    dve.wait_ge(o_a, ev(1, b))
                    dve.tensor_tensor(ot[:, s], ot[:, s], er[:, s, 0], ALU.add).then_inc(o_b, 1)

        @block.tensor
        def _(pe):
            start_ahead(pe, (n_xT, 1), (n_qk, 4), (n_lg, 1), (a_u, U), (a_v, 2), (a_s, 4), (a_T, 2), (a_G, 1),
                        (a_xT, 1), (a_num, 4), (f_xT, 1), (f_g, 1), (f_u, 1))
            start_ahead(pe, (a_nT, 4), (a_y, 1), (f_aT, 1), (f_y, 1), tail=1)

            def split3(dst, ah, al, bh, bl, start=True, stop=True):
                pe.matmul(dst, ah, bh, start=start, stop=False)
                pe.matmul(dst, al, bh, start=False, stop=False)
                return pe.matmul(dst, ah, bl, start=False, stop=stop)

            pe.wait_ge(w_in[3], 16)
            pe.wait_ge(s_ctr, 3)
            pe.wait_ge(s_const, 1)
            natural = {"q": wqn, "k": wkn, "v": wvn, "o": won}
            los = 0
            for j, (kind, n) in enumerate(SETUP):
                if j >= 4:
                    pe.wait_ge(s_trh, j - 3)
                    if SETUP[j - 4][0] in "qkv":
                        los += 1
                        pe.wait_ge(s_trl, los)
                for i in range(4):
                    dst = bank[j % 4][:, P * i:P * i + P]
                    if kind == "M":
                        h = 8 * (n // 2) + n % 2 + 2 * i
                        r = slice(DH * (h % 2), DH * (h % 2) + DH)
                        last = pe.matmul(dst, wqn[r, h // 2, :], wkn[r, h // 2, :], start=True, stop=True)
                    else:
                        last = pe.transpose(dst, natural[kind][:, 4 * n + i, :], ident[:])
                last.then_inc(s_tr, 1)
            pe.wait_ge(s_trh, len(SETUP))
            pe.wait_ge(s_trl, 6)
            pe.wait_ge(w_in[4], 16)

            def xT_for_norms(c, s):
                pe.wait_ge(n_xn, ev(1, c))
                pe.wait_ge(n_xTl, ev(1, c - 2))
                pe.transpose(bank[4 + s][:, 0:P], xn[:, s, 0:D], ident[:]).then_inc(n_xT, 1)

            xT_for_norms(0, 0)
            with pe.Fori(0, C // 2) as c2:
                for s in range(2):
                    c = c2 * 2 + s
                    pe.wait_ge(n_xTl, ev(1, c))
                    for j in range(4):
                        pe.wait_ge(n_sq, ev(4, c - 1, j))
                        w = slice(512 * j, 512 * j + 512)
                        split3(bank[j][:], xTh[:, s, 0:P], xTl[:, s, 0:P], WNh[:, w], WNl[:, w]).then_inc(n_qk, 1)
                        if j == 1:
                            xT_for_norms(c + 1, 1 - s)
                    pe.wait_ge(n_lc, ev(1, c - 2))
                    pe.matmul(bank[6 + s][:, 0:E], xTf[:, s, :], rwf[:], start=True, stop=True).then_inc(n_lg, 1)
            pe.wait_ge(r_oh, 2)
            pe.wait_ge(n_sq, ev(4, C - 1, 3))
            for k in range(K2):
                pe.matmul(bank[k][:], before[:], ohb[:, k].rearrange("p c e -> p (c e)"), start=True, stop=True)
                last = pe.matmul(bank[2 + k][:], ones[:], ohb[:, k].rearrange("p c e -> p (c e)"), start=True, stop=True)
            last.then_inc(r_cnt, 1)
            barrier(pe, 1)

            def transpose_x(c, r, p=None):
                if p is not None:
                    wait_wide(pe, p, "x", 2 + r % 2)
                pe.wait_ge(e_xn, ev(1, c))
                pe.transpose(wide("x", 2 + r % 2)[:, 0:P], xn[:, r % 4, 0:D], ident[:]).then_inc(a_xT, 1)

            def u(p, pr, g):
                wait_wide(pe, p, "u", 0, g)
                for n in range(2):
                    last = split3(wide("u", 0, g)[:, 2 * P * n:2 * P * n + 2 * P],
                                  Mh[:, 2 * g + n, :], Ml[:, 2 * g + n, :], xTh[:, pr, :], xTl[:, pr, :])
                last.then_inc(a_u, 1)

            def v(p, pr, s, n):
                wait_wide(pe, p, "v", s, n)
                w, t = slice(512 * n, 512 * n + 512), slice(P * s, P * s + P)
                split3(wide("v", s, n)[:], xTh[:, pr, t], xTl[:, pr, t], Wvh[:, w], Wvl[:, w]).then_inc(a_v, 1)

            def scores(p, pr, s, q):
                wait_wide(pe, p, "s", s, q)
                pe.wait_ge(e_ul, ev(U, p, 2 * q + 1))
                t = slice(P * s, P * s + P)
                split3(wide("s", s, q)[:].rearrange("p (h i) -> p h i", i=P), xTh[:, pr, t], xTl[:, pr, t],
                       uh[:, 2 * q:2 * q + 2, :, t].rearrange("p g h i -> p (g h) i"),
                       ul[:, 2 * q:2 * q + 2, :, t].rearrange("p g h i -> p (g h) i")).then_inc(a_s, 1)

            def T(p, s, n):
                wait_wide(pe, p, "T", s, n)
                w = slice(512 * n, 512 * n + 512)
                pe.wait_ge(e_Gs, 2 * p + s + 1)
                split3(wide("T", s, n)[:], Gh[:, 0:D], Gl[:, 0:D], Wvh[:, w], Wvl[:, w]).then_inc(a_T, 1)

            def G(p, pr, s):
                wait_wide(pe, p, "G", s)
                x_ = xn[:, 2 * pr + s, :]
                pe.matmul(wide("G", s)[:, 0:D + 2], x_[:, 0:D], x_, start=True, stop=True).then_inc(a_G, 1)

            def num(p, s, q):
                c = 2 * p + s
                pe.wait_ge(e_nn, ev(4, c, q - 2) if q >= 2 else ev(4, c - 1, q + 2))
                pe.wait_ge(e_v, ev(2, c, q // 2))
                pe.wait_ge(e_T, ev(2, c, q // 2))
                pe.wait_ge(e_A, ev(4, c, q))
                for i in range(HQ):
                    h = HQ * q + i
                    o = bank[4 + q % 2][:, VE * i:VE * i + VE]
                    pe.matmul(o, Am[:, q, i, :], vx[:, s, h, :], start=True, stop=False)
                    last = pe.matmul(o, uf[:, h // 2, h % 2, P * s:P * s + P], Tx[:, s, h, :], start=False, stop=True)
                last.then_inc(a_num, 1)

            def transpose_num(c, s, q):
                pe.wait_ge(e_nn, ev(4, c, q))
                pe.wait_ge(e_nT, ev(4, c, q - 1) if q else ev(4, c - 1, 3))
                for t in range(2):
                    last = pe.transpose(bank[6][:, P * t:P * t + P],
                                        nn[:, s, q, 2 * t:2 * t + 2, :].rearrange("p h e -> p (h e)"), ident[:])
                last.then_inc(a_nT, 1)

            def y(c, q):
                if q == 0:
                    pe.wait_ge(e_y, ev(1, c - 1))
                pe.wait_ge(e_nT, ev(4, c, q))
                for t in range(2):
                    last = pe.matmul(bank[7][:, 0:D], nT[:, q, t, :], WoT[:, 2 * q + t, :],
                                     start=(q == 0 and t == 0), stop=(q == Q - 1 and t == 1))
                if q == Q - 1:
                    last.then_inc(a_y, 1)

            transpose_x(0, 0)
            transpose_x(1, 1)
            with pe.Fori(0, B) as b:
                pe.wait_ge(s_new, b + 1)
                pe.sem_inc(s_pass, 1)
                with pe.Fori(0, CB // 4) as half:
                    for pr in range(2):
                        p = b * (CB // 2) + half * 2 + pr
                        A, Z = 2 * p, 2 * p - 1

                        def u_(g):
                            pe.wait_ge(e_M, ev(U, b, g))
                            u(p, pr, g)

                        pe.wait_ge(e_xTl, ev(1, A + 1))
                        u_(0)
                        u_(1)
                        transpose_num(Z, 1, 0)
                        u_(2)
                        u_(3)
                        transpose_num(Z, 1, 1)
                        v(p, pr, 0, 0)
                        scores(p, pr, 0, 0)
                        y(Z, 0)
                        u_(4)
                        scores(p, pr, 0, 1)
                        transpose_num(Z, 1, 2)
                        T(p, 0, 0)
                        y(Z, 1)
                        u_(5)
                        num(p, 0, 0)
                        v(p, pr, 0, 1)
                        scores(p, pr, 0, 2)
                        transpose_num(Z, 1, 3)
                        T(p, 0, 1)
                        num(p, 0, 1)
                        u_(6)
                        y(Z, 2)
                        u_(7)
                        G(p, pr, 0)
                        num(p, 0, 2)
                        y(Z, 3)
                        scores(p, pr, 0, 3)
                        v(p, pr, 1, 0)
                        scores(p, pr, 1, 0)
                        num(p, 0, 3)
                        v(p, pr, 1, 1)
                        scores(p, pr, 1, 1)
                        T(p, 1, 0)
                        transpose_num(A, 0, 0)
                        num(p, 1, 0)
                        scores(p, pr, 1, 2)
                        T(p, 1, 1)
                        transpose_num(A, 0, 1)
                        y(A, 0)
                        num(p, 1, 1)
                        scores(p, pr, 1, 3)
                        transpose_num(A, 0, 2)
                        y(A, 1)
                        num(p, 1, 2)
                        G(p, pr, 1)
                        transpose_x(A + 2, 2 * pr + 2, p)
                        transpose_num(A, 0, 3)
                        y(A, 2)
                        transpose_x(A + 3, 2 * pr + 3, p)
                        y(A, 3)
                        num(p, 1, 3)
            for q in range(Q):
                transpose_num(C - 1, 1, q)
                y(C - 1, q)
            barrier(pe, 2)

            pe.wait_ge(f_ms, 2)
            pe.wait_ge(f_wl, E)
            pe.wait_ge(f_dn, 32 * E)

            def transpose_tile(i, r):
                pe.wait_ge(f_xTl, ev(1, i - 1))
                pe.transpose(bank[0][:, 0:P], xt[:, r, 0:D], ident[:]).then_inc(f_xT, 1)

            def gate_up(i, s, ex, g, free, done):
                pe.wait_ge(free, ev(1, i - 2))
                wh = guh[:, bass.ds(ex, 1), g, :].rearrange("p a f -> p (a f)")
                wl = gul[:, bass.ds(ex, 1), g, :].rearrange("p a f -> p (a f)")
                split3(bank[1 + 2 * g + s][:, 0:F], xtTh[:, s, :], xtTl[:, s, :], wh, wl).then_inc(done, 1)

            def transpose_hidden(i, s):
                pe.wait_ge(f_act, ev(1, i))
                pe.wait_ge(f_aTc, ev(1, i - 1))
                for t in range(FT):
                    last = pe.transpose(bank[5][:, P * t:P * t + P], act_[:, s, P * t:P * t + P], ident[:])
                last.then_inc(f_aT, 1)

            def down_(i, s, ex):
                pe.wait_ge(f_aTc, ev(1, i))
                pe.wait_ge(f_yt, ev(1, i - 2))
                for t in range(FT):
                    last = pe.matmul(bank[6 + s][:, 0:D], aT[:, s, t, :], dn[:, bass.ds(ex, 1), t, :].rearrange("p a f -> p (a f)"),
                                     start=(t == 0), stop=(t == FT - 1))
                last.then_inc(f_y, 1)

            pe.wait_ge(f_xt[0], 16)
            transpose_tile(0, 0)
            with pe.Fori(0, TILES // RT) as i4:
                ex_before = pe.value_load(tile_e[0:1, bass.ds(i4 * RT, 1)], min_val=0, max_val=E - 1)
                for r in range(RT):
                    i, s = i4 * RT + r, r % 2
                    ex = pe.value_load(tile_e[0:1, bass.ds(i + 1, 1)], min_val=0, max_val=E - 1)
                    pe.wait_ge(f_xTl, ev(1, i))
                    gate_up(i, s, ex, 0, f_sl, f_g)
                    transpose_hidden(i - 1, 1 - s)
                    gate_up(i, s, ex, 1, f_act, f_u)
                    down_(i - 1, 1 - s, ex_before)
                    pe.wait_ge(f_xt[(r + 1) % RT], 16 * (i4 + 1) if r < RT - 1 else 16 * (i4 + 2))
                    transpose_tile(i + 1, (r + 1) % RT)
                    ex_before = ex
            transpose_hidden(TILES - 1, 1)
            down_(TILES - 1, 1, pe.value_load(tile_e[0:1, TILES:TILES + 1], min_val=0, max_val=E - 1))
            barrier(pe, 3)


_INS = ["L0_attn_X", "L0_attn_Wq", "L0_attn_Wk", "L0_attn_Wv", "L0_attn_Wo", "L0_attn_bo",
        "L0_ffn_router_w", "L0_ffn_gate_proj", "L0_ffn_up_proj", "L0_ffn_down_proj"]


def kernel(**inputs):
    import numpy as np
    import concourse.bacc as bacc
    from concourse import mybir as mb
    from concourse.bass_utils import run_bass_kernel_spmd as run

    nc = bacc.Bacc("TRN2", target_bir_lowering=False, num_devices=1)
    arrays, args = {}, []
    for name in _INS:
        a = np.ascontiguousarray(inputs[name])
        arrays[f"in_{name}"] = a
        args.append(nc.dram_tensor(f"in_{name}", a.shape, mb.dt.from_np(a.dtype), kind="ExternalInput").ap())
    args.append(nc.dram_tensor("out_0", (C, P, D), mb.dt.float32, kind="ExternalOutput").ap())
    build(nc, *args)
    r = run(nc, [arrays], core_ids=[0])
    return r.results[0]["out_0"].reshape(B, N, D)
```

```python
import concourse.bass as bass
from concourse import mybir
from contextlib import ExitStack

B, N, D = 8, 1024, 128
H, DH = 16, 64
E, F = 8, 352
P = 128
C = B * N // P
CB = N // P
Q, HQ = 4, H // 4
NJ = 5
U = 8
VE = D + 1
K2 = 2
TILES = K2 * C + E
SLOTS = (TILES + 2) * P
ROW = D + 4
DST, WGT = D, D + 1
SPARE = 2 * E + 1
RT = 8
OB = 4
FT = 3
AHEAD = 8
EPS = 1e-5


def build(nc, x, wq, wk, wv, wo, bo, rw, gate, up, down, out):
    f32, f32r, bf16 = mybir.dt.float32, mybir.dt.float32r, mybir.dt.bfloat16
    i32 = mybir.dt.int32
    ALU, ACT, AX = mybir.AluOpType, mybir.ActivationFunctionType, mybir.AxisListType

    xs_d = nc.dram_tensor("sorted_tokens", (SLOTS, ROW), f32, kind="Internal").ap()
    ys_d = nc.dram_tensor("expert_rows", (K2 * B * N + SPARE * P, D), f32, kind="Internal").ap()

    ctx = ExitStack()
    with ctx:
        at = [nc.sbuf_base]

        def place(name, shape, dt=f32, size=4):
            n = size
            for d in shape[1:]:
                n *= d
            t = nc.alloc_sbuf_tensor_at(name, shape, dt, offset=at[0])
            at[0] += -(-n // 32) * 32
            return t

        at[0] = -(-at[0] // 32) * 32
        xa = place("xa", [P, C + 3, D])
        rstd = place("rstd", [P, C + 3])
        nmr = place("nmr", [P, C + 3])
        nmr1 = place("nmr1", [P, C + 3])
        xn = place("xn", [P, 4, D])
        xTh, xTl = place("xTh", [P, 2, 2 * P], f32r), place("xTl", [P, 2, 2 * P], f32r)
        ident = place("ident", [P, P])
        causal = place("causal", [P, P])
        blank = place("blank", [P, SPARE, ROW])
        bob = place("bob", [P, D])
        Mf = place("Mf", [P, H, D])
        Mt = place("Mt", [P, 2, D])
        Wx = place("Wx", [P, H, VE])
        cc = place("cc", [P, B + 1, H])
        slot = place("slot", [P, C, K2], i32)
        meta = place("meta", [P, C, K2, 2])
        pad = place("pad", [P, E], i32)
        dump = place("dump", [P, 1], i32)
        tile_e = place("tile_e", [P, TILES + 3], i32)
        iot = place("iot", [P, TILES])
        endt = place("endt", [P, E])
        sidx = place("sidx", [P, 2, K2], i32)
        pay = place("pay", [P, 2, K2, ROW])
        shared = at[0]
        WNh, WNl = place("WNh", [P, 2 * H * DH + E], f32r), place("WNl", [P, 2 * H * DH + E], f32r)
        rwf = place("rwf", [P, E])
        mv = place("mv", [P, C, 2])
        wmean = place("wmean", [P, 3, 8])
        t64 = place("t64", [P, 2, C])
        before = place("before", [P, P], bf16, 2)
        ones = place("ones", [P, P], bf16, 2)
        onesf = place("onesf", [P, P])
        Mt0 = place("Mt0", [P, 2, 2, D])
        WoT = place("WoT", [P, 8, D])
        wqn, wkn, wvn, won = (place(n, [P, 8, D]) for n in ("wqn", "wkn", "wvn", "won"))
        sq = place("sq", [P, NJ, 7 * DH])
        ssq = place("ssq", [P, C, 2 * H])
        mx = place("mx", [P, B, 2 * H])
        mxa = place("mxa", [P, B, 2 * H])
        ra, rb = place("ra", [P, B, 2 * H]), place("rb", [P, B, 2 * H])
        L = place("L", [P, C, E])
        L2 = place("L2", [P, C, E])
        eqw = place("eqw", [P, C, E])
        oh = place("oh", [P, K2, C, E])
        ohb = place("ohb", [P, K2, C, E], bf16, 2)
        pre = place("pre", [P, K2 * C + 1, E])
        posn = place("posn", [P, K2 * C, E])
        slf = place("slf", [P, K2 * C])
        m1, m2, mm = place("m1", [P, C]), place("m2", [P, C]), place("mm", [P, C])
        wtop = place("wtop", [P, K2, C])
        ord8 = place("ord8", [P, E])
        cnt, til, base = (place(n, [P, E]) for n in ("cnt", "til", "base"))
        cnti = place("cnti", [P, E], i32)
        iop = place("iop", [P, 1])
        padf = place("padf", [P, E])
        end1 = at[0]
        at[0] = shared
        Mh, Ml = zip(*((place(f"Mh{n}", [P, H, D], f32r), place(f"Ml{n}", [P, H, D], f32r)) for n in range(2)))
        uh, ul = place("uh", [P, U, 2, 2 * P], f32r), place("ul", [P, U, 2, 2 * P], f32r)
        Am = place("Am", [P, 2, HQ, P])
        Ah, Al = place("Ah", [P, Q, HQ, P], f32r), place("Al", [P, Q, HQ, P], f32r)
        xh, xl = place("xh", [P, 4, D], f32r), place("xl", [P, 4, D], f32r)
        zf = place("zf", [P, 2, HQ, P])
        Gf = place("Gf", [P, D])
        Gh, Gl = place("Gh", [P, 2, D], f32r), place("Gl", [P, 2, D], f32r)
        rden = place("rden", [P, Q, 2, 2])
        acc = place("acc", [P, 2, HQ, D])
        ysum = place("ysum", [P, 2, D])
        end2 = at[0]
        at[0] = shared
        guh, gul = place("guh", [P, E, 2, F], f32r), place("gul", [P, E, 2, F], f32r)
        xt = place("xt", [P, RT, ROW])
        xtTh, xtTl = place("xtTh", [P, 2, P], f32r), place("xtTl", [P, 2, P], f32r)
        wd = place("wd", [P, RT, 2])
        wdi = place("wdi", [P, RT], i32)
        sl = place("sl", [P, 2, F])
        act_ = place("act_", [P, 2, FT * P])
        aT = place("aT", [P, 2, FT, P])
        yt = place("yt", [P, RT, D])
        ge = place("ge", [P, TILES, E])
        tef = place("tef", [P, TILES])
        end3 = at[0]
        at[0] = shared
        er = place("er", [P, OB, K2, CB, D])
        ot = place("ot", [P, OB, CB, D])
        end4 = at[0]
        top = nc.sbuf_usable_end // 32 * 32 - 4 * E * (2 * F + FT * D)
        at[0] = top
        gu = place("gu", [P, E, 2, F])
        dn = place("dn", [P, E, FT, D])
        assert max(end1, end2, end3, end4) <= top and at[0] <= nc.sbuf_usable_end, (end1, end2, end3, end4, top)

        bank = [ctx.enter_context(nc.psum_tensor(f"bank{n}", [P, 512], f32)) for n in range(4)]
        ybank = [ctx.enter_context(nc.psum_tensor(f"ybank{n}", [P, 2, 512], f32)) for n in range(2)]
        bank += [ybank[n][:, m] for n in range(2) for m in range(2)]

        sems = {}

        def sem(name):
            sems[name] = ctx.enter_context(nc.semaphore(name))
            return sems[name]

        phase = sem("phase")
        s_pass = sem("s_pass")
        x_in, w_in, bo_in = [sem(f"x_in{n}") for n in range(8)], [sem(f"w_in{n}") for n in range(5)], sem("bo_in")
        s_ctr = sem("s_ctr")
        s_const, s_pool = sem("s_const"), sem("s_pool")
        s_tr, s_trh, s_trl = sem("s_tr"), sem("s_trh"), sem("s_trl")
        s_late, s_lateh, s_bs = sem("s_late"), sem("s_lateh"), sem("s_bs")
        s_stat, s_chain, s_rt, s_sqrt = sem("s_stat"), sem("s_chain"), sem("s_rt"), sem("s_sqrt")
        s_rw = sem("s_rw")
        n_xn, n_xT, n_xTh, n_xTl = sem("n_xn"), sem("n_xT"), sem("n_xTh"), sem("n_xTl")
        n_qk, n_sq, n_red, n_lc = sem("n_qk"), sem("n_sq"), sem("n_red"), sem("n_lc")
        s_mx, s_all = sem("s_mx"), sem("s_all")
        r_oh, r_cnt = sem("r_oh"), sem("r_cnt")
        z_tail, z_out, c_xn, c_idx = sem("z_tail"), sem("z_out"), sem("c_xn"), sem("c_idx")
        c_out = [sem("c_out0"), sem("c_out1")]
        a_u, a_s, a_z, a_Y, a_G, a_xT = (sem(f"a_{n}") for n in ("u", "s", "z", "Y", "G", "xT"))
        e_uh, e_ul, e_Am, e_Ah, e_Al, e_z, e_r, e_Y, e_sum, e_y, e_G, e_Gs, e_xn, e_xh, e_xl, e_xTh, e_xTl, e_M = (
            sem(f"e_{n}") for n in ("uh", "ul", "Am", "Ah", "Al", "z", "r", "Y", "sum", "y", "G", "Gs",
                                    "xn", "xh", "xl", "xTh", "xTl", "M"))
        s_cc, s_pad = sem("s_cc"), sem("s_pad")
        s_Mt, s_Mh, s_gh, s_new, s_dummy = sem("s_Mt"), sem("s_Mh"), sem("s_gh"), sem("s_new"), sem("s_dummy")
        f_w, f_wh, f_wl = sem("f_w"), sem("f_wh"), sem("f_wl")
        f_dn, f_dz = sem("f_dn"), sem("f_dz")
        f_xt, f_sc = [sem(f"f_xt{n}") for n in range(RT)], [sem(f"f_sc{n}") for n in range(RT)]
        f_xT, f_xTh, f_xTl, f_wd, f_wi, f_g, f_u, f_sl, f_act, f_aT, f_aTc, f_y, f_yt = (
            sem(f"f_{n}") for n in
            ("xT", "xTh", "xTl", "wd", "wi", "g", "u", "sl", "act", "aT", "aTc", "y", "yt"))
        o_in, o_out = [sem(f"o_in{n}") for n in range(OB)], [sem(f"o_out{n}") for n in range(OB)]
        o_a, o_b = sem("o_a"), sem("o_b")
        f_ms, f_te = sem("f_ms"), sem("f_te")

        def ev(n, c, k=0):
            return n * (c + AHEAD) + k + 1

        def start_ahead(eng, *pairs, spare=0):
            for s, n in pairs:
                eng.sem_inc(s, n * AHEAD - spare)

        def barrier(eng, n):
            eng.drain().then_inc(phase, 1)
            eng.wait_ge(phase, 5 * n)

        JOBS = [("u", 0, 0), ("u", 0, 1), ("z", -1, 2), ("u", 0, 2), ("u", 0, 3), ("s", 0, 0),
                ("u", 0, 4), ("z", -1, 3), ("u", 0, 5), ("s", 0, 1),
                ("u", 0, 6), ("z", 0, 0), ("u", 0, 7), ("s", 0, 2), ("G", 0, 0),
                ("z", 0, 1), ("s", 0, 3), ("s", 1, 0), ("z", 0, 2),
                ("s", 1, 1), ("z", 0, 3), ("x", 2, 0), ("s", 1, 2), ("z", 1, 0), ("x", 3, 0), ("G", 1, 0),
                ("s", 1, 3), ("z", 1, 1)]
        FREED = {"u": (e_ul, U), "s": (e_Am, 4), "z": (e_z, 4), "G": (e_G, 1), "x": (e_xTl, 1)}

        def wide(kind, r, k=0):
            return bank[JOBS.index((kind, r, k)) % 4]

        def wait_wide(eng, p, kind, r, k=0):
            j = JOBS.index((kind, r, k)) - 4
            kind4, r4, k4 = JOBS[j]
            s, n = FREED[kind4]
            p4 = p if j >= 0 else p - 1
            eng.wait_ge(s, ev(n, p4 if kind4 == "u" else 2 * p4 + r4, k4))

        ROUTER = 2 * H * DH

        def job_columns(j):
            return slice(7 * DH * j, min(7 * DH * (j + 1), ROUTER + E))

        def job_heads(j):
            return slice(7 * j, min(7 * (j + 1), 2 * H))

        def heads_width(j):
            return DH * (job_heads(j).stop - job_heads(j).start)

        jbank = [*bank[0:4], bank[6]]

        SETUP = [(t, n) for t in "qk" for n in range(2)]
        LATE = [("M", n) for n in range(4)] + [("o", n) for n in range(2)] + [("W", n) for n in range(4)]

        def heads_of(n):
            h0 = 8 * (n // 2) + n % 2
            return slice(h0, h0 + 7, 2)

        block = ctx.enter_context(nc.Block())

        @block.sync
        def _(sp):
            sp.dma_start(rwf[:], rw).then_inc(w_in[4], 16)
            for n, (t, src) in enumerate(((wqn, wq), (wkn, wk))):
                sp.dma_start(t[:], src.rearrange("(t p) d -> p t d", p=P)).then_inc(w_in[n], 16)
            for n in range(8):
                sp.dma_start(xa[:, 1 + n * CB:1 + (n + 1) * CB, :],
                             x[n].rearrange("(c p) d -> p c d", p=P)).then_inc(x_in[n], 16)
            sp.dma_start(wvn[:], wv.rearrange("(t p) d -> p t d", p=P)).then_inc(w_in[2], 16)
            sp.dma_start(won[:], wo.rearrange("o (t d) -> o t d", d=D)).then_inc(w_in[3], 16)
            sp.dma_start(bob[:], bo.rearrange("(a d) -> a d", a=1).broadcast_to([P, D])).then_inc(bo_in, 16)
            sp.dma_start(gu[:, :, 0, :], gate.rearrange("e d f -> d e f")).then_inc(f_w, 16)
            sp.dma_start(gu[:, :, 1, :], up.rearrange("e d f -> d e f")).then_inc(f_w, 16)
            sp.wait_ge(f_dz, 1)
            for e in range(E):
                sp.dma_start(dn[:, e, 0:2, :], down[e, 0:256, :].rearrange("(t p) d -> p t d", p=P)).then_inc(f_dn, 16)
                sp.dma_start(dn[0:F - 256, e, 2, :], down[e, 256:F, :]).then_inc(f_dn, 16)
            sp.wait_ge(s_const, 7)
            sp.dma_start(xs_d[(K2 * C + 1) * P:SLOTS, :].rearrange("(t p) d -> p t d", p=P),
                         blank[:, E:SPARE, :]).then_inc(z_tail, 16)
            sp.wait_ge(z_tail, 16)
            sp.wait_ge(bo_in, 16)
            barrier(sp, 1)
            barrier(sp, 2)
            def load_tile(i, r):
                sp.dma_start(xt[:, r, :], xs_d[bass.ds((i + 1) * P, P), :]).then_inc(f_xt[r], 16)

            load_tile(0, 0)
            with sp.Fori(0, TILES // RT) as i4:
                for r in range(RT):
                    i = i4 * RT + r
                    sp.wait_ge(f_xT, ev(1, i - 3))
                    sp.wait_ge(f_wd, ev(1, i - 3))
                    load_tile(i + 1, (r + 1) % RT)
            barrier(sp, 3)
            with sp.Fori(0, B // OB) as b4:
                for s in range(OB):
                    b = b4 * OB + s
                    sp.wait_ge(o_b, ev(1, b - OB))
                    for k in range(K2):
                        sp.dma_start(er[:, s, k], ys_d[bass.ds((b + B * k) * N, N), :].rearrange("(c p) d -> p c d", p=P)
                                     ).then_inc(o_in[s], 16)
            for s in range(OB):
                sp.wait_ge(o_out[s], 16 * (B // OB + 1))

        @block.gpsimd
        def _(pool):
            start_ahead(pool, (e_M, U), (e_Al, 4), (e_xl, 1), (e_sum, 1), (o_a, 1), (f_wi, 1))
            start_ahead(pool, (e_y, 1), spare=1)
            for t in o_out:
                pool.sem_inc(t, 16)
            pool.memset(blank[:], 0.0).then_inc(s_pool, 1)
            pool.memset(ident[:], 0.0).then_inc(s_pool, 1)
            pool.memset(causal[:], 1.0).then_inc(s_pool, 1)
            pool.memset(onesf[:], 1.0).then_inc(s_pool, 1)
            pool.memset(before[:], 1.0).then_inc(s_pool, 1)
            pool.memset(ones[:], 1.0).then_inc(s_pool, 1)
            pool.memset(cc[:, B, :], 1.0).then_inc(s_pool, 1)
            for t in (xa[:, 0, :], xa[:, C + 1:C + 3, :], rstd[:, C + 1:C + 3], nmr[:, C + 1:C + 3], nmr1[:, C + 1:C + 3],
                      pay[:, :, :, D + 2:ROW]):
                pool.memset(t, 0.0).then_inc(s_pool, 1)
            pool.memset(dn[:, :, FT - 1, :], 0.0).then_inc(f_dz, 1)
            pool.wait_ge(s_pool, 13)
            pool.affine_select(out=ident[:], in_=ident[:], compare_op=ALU.not_equal, fill=1.0,
                               base=0, pattern=[[-1, P]], channel_multiplier=1).then_inc(s_const, 1)
            pool.affine_select(out=causal[:], in_=causal[:], compare_op=ALU.is_ge, fill=0.0,
                               base=0, pattern=[[1, P]], channel_multiplier=-1).then_inc(s_const, 1)
            pool.affine_select(out=before[:], in_=before[:], compare_op=ALU.is_gt, fill=0.0,
                               base=0, pattern=[[1, P]], channel_multiplier=-1).then_inc(s_const, 1)
            pool.iota(ord8[:], pattern=[[-1, E]], base=E, channel_multiplier=0,
                      allow_small_or_imprecise_dtypes=True).then_inc(s_const, 1)
            pool.iota(iot[:], pattern=[[1, TILES]], base=0, channel_multiplier=0,
                      allow_small_or_imprecise_dtypes=True).then_inc(s_const, 1)
            pool.iota(iop[:], pattern=[[0, 1]], base=0, channel_multiplier=1,
                      allow_small_or_imprecise_dtypes=True).then_inc(s_const, 1)
            pool.iota(blank[:, :, DST], pattern=[[P, SPARE]], base=K2 * B * N, channel_multiplier=1,
                      allow_small_or_imprecise_dtypes=True).then_inc(s_const, 1)
            pool.iota(dump[:], pattern=[[0, 1]], base=K2 * B * N, channel_multiplier=1).then_inc(s_const, 1)
            pool.iota(meta[:, :, :, 0], pattern=[[P, C], [B * N, K2]], base=0, channel_multiplier=1,
                      allow_small_or_imprecise_dtypes=True).then_inc(s_const, 1)
            pool.wait_ge(s_const, 9)
            for n in range(2):
                for r in range(RT):
                    pool.indirect_dma_start(ys_d, bass.IndirectOffsetOnAxis(ap=dump[:], axis=0),
                                            blank[:, 0, 0:D], None).then_inc(f_sc[r], 16)
                    pool.wait_ge(f_sc[r], 16 * (n + 1))
            pool.wait_ge(s_mx, 1)
            pool.partition_all_reduce(mxa[:].rearrange("p b h -> p (b h)"), mx[:].rearrange("p b h -> p (b h)"),
                                      P, bass.bass_isa.ReduceOp.max).then_inc(s_all, 1)

            def scale_M(b, bp, g):
                hs = bass.ds(2 * g, 2)
                pool.tensor_tensor(Mt[:], Mf[:, hs, :],
                                   cc[:, bass.ds(b, 1), hs].rearrange("p a h -> p (a h)").unsqueeze(2).broadcast_to([P, 2, D]),
                                   ALU.mult).then_inc(s_Mt, 1)
                pool.wait_ge(s_Mt, U * b + g + 1)
                pool.wait_ge(a_u, ev(U, 4 * b - 5, g))
                pool.sem_inc(s_pass, 1)
                pool.tensor_copy(Mh[bp][:, hs, :], Mt[:]).then_inc(s_Mh, 1)
                pool.wait_ge(s_Mh, U * b + g + 1)
                pool.tensor_tensor(Ml[bp][:, hs, :], Mt[:], Mh[bp][:, hs, :], ALU.subtract).then_inc(e_M, 1)
                pool.wait_ge(e_M, ev(U, b, g))

            def scatter(c, s):
                pool.wait_ge(c_xn, c + 1)
                pool.sem_inc(s_pass, 1)
                pool.tensor_copy(sidx[:, s, :], slot[:, bass.ds(c, 1), :].rearrange("p a k -> p (a k)")).then_inc(c_idx, 1)
                pool.tensor_copy(pay[:, s, :, D:D + 2], meta[:, bass.ds(c, 1)].rearrange("p a k m -> p (a k) m")).then_inc(c_idx, 1)
                pool.wait_ge(c_idx, 2 * c + 2)
                pool.sem_inc(s_pass, 1)
                for k in range(K2):
                    pool.indirect_dma_start(
                        xs_d, bass.IndirectOffsetOnAxis(ap=sidx[:, s, k:k + 1], axis=0),
                        pay[:, s, k, :], None).then_inc(c_out[s], 16)

            def scores_lo(c, q):
                pool.wait_ge(e_Ah, ev(4, c, q))
                pool.tensor_tensor(Al[:, q], Am[:, q % 2], Ah[:, q], ALU.subtract).then_inc(e_Al, 1)

            def x_lo(c, r):
                pool.wait_ge(e_xh, ev(1, c))
                pool.tensor_tensor(xl[:, r % 4], xn[:, r % 4], xh[:, r % 4], ALU.subtract).then_inc(e_xl, 1)

            def y_add(c, s):
                pool.wait_ge(e_y, ev(1, c - 1))
                pool.wait_ge(e_Y, ev(4, c, 3))
                pool.tensor_tensor(ysum[:], acc[:, s, 0:2], acc[:, s, 2:4], ALU.add).then_inc(e_sum, 1)
                pool.wait_ge(e_sum, AHEAD + c + 2)
                pool.tensor_tensor(xa[:, bass.ds(c + 1, 1), :].rearrange("p a d -> p (a d)"),
                                   ysum[:, 0], ysum[:, 1], ALU.add).then_inc(e_y, 1)

            def attend_pair(p, pr, b, bp, half):
                A = 2 * p
                scores_lo(A, 0)
                scale_M(b + 1, 1 - bp, 4 * half + 2 * pr)
                scores_lo(A, 1)
                scatter(A, 0)
                scores_lo(A, 2)
                y_add(A - 1, 1)
                scores_lo(A, 3)
                x_lo(A + 2, 2 * pr + 2)
                scores_lo(A + 1, 0)
                x_lo(A + 3, 2 * pr + 3)
                scores_lo(A + 1, 1)
                scatter(A + 1, 1)
                scores_lo(A + 1, 2)
                scale_M(b + 1, 1 - bp, 4 * half + 2 * pr + 1)
                scores_lo(A + 1, 3)
                y_add(A, 0)

            pool.wait_ge(s_cc, 1)
            for g in range(U + 1):
                if g < U:
                    if g >= 2:
                        pool.wait_ge(e_M, ev(U, 0, g - 2))
                    pool.tensor_tensor(Mt0[:, g % 2], Mf[:, 2 * g:2 * g + 2, :],
                                       cc[:, 0, 2 * g:2 * g + 2].unsqueeze(2).broadcast_to([P, 2, D]),
                                       ALU.mult).then_inc(s_Mt, 1)
                if g > 0:
                    hs = slice(2 * g - 2, 2 * g)
                    pool.wait_ge(s_Mh, g)
                    pool.tensor_tensor(Ml[0][:, hs, :], Mt0[:, (g - 1) % 2], Mh[0][:, hs, :], ALU.subtract).then_inc(e_M, 1)
            pool.drain().then_inc(phase, 1)
            pool.wait_ge(s_pad, 1)
            pool.wait_ge(z_tail, 16)
            for e in range(E):
                pool.indirect_dma_start(xs_d, bass.IndirectOffsetOnAxis(ap=pad[:, e:e + 1], axis=0),
                                        blank[:, e, :], None).then_inc(z_out, 16)
            pool.wait_ge(phase, 5)
            for t, v in ((Al[:, 2:4].bitcast(f32), 0.0), (ul[:, 4:8, :, P:2 * P].bitcast(f32), 0.0), (zf[:, 1], 1.0)):
                pool.memset(t, v).then_inc(s_dummy, 1)
            x_lo(0, 0)
            x_lo(1, 1)
            pool.wait_ge(z_out, 16 * E)
            with pool.Fori(0, B // 2) as b2:
                for bp in range(2):
                    b = b2 * 2 + bp
                    with pool.Fori(0, CB // 4) as half:
                        for pr in range(2):
                            attend_pair(b * (CB // 2) + half * 2 + pr, pr, b, bp, half)
            y_add(C - 1, 1)
            for s in range(2):
                pool.wait_ge(c_out[s], 16 * K2 * (C // 2))
            barrier(pool, 2)

            pool.memset(act_[:], 0.0).then_inc(f_ms, 1)
            pool.memset(wd[:], 0.0).then_inc(f_ms, 1)
            pool.memset(aT[:], 0.0).then_inc(f_ms, 1)
            for e in range(E - 3, E):
                pool.wait_ge(f_wh, e - (E - 3) + 1)
                pool.tensor_tensor(gul[:, e], gu[:, e], guh[:, e], ALU.subtract).then_inc(f_wl, 1)
            with pool.Fori(0, TILES // RT) as i4:
                for r in range(RT):
                    i = i4 * RT + r
                    pool.wait_ge(f_sc[r], 16 * (i4 + 2))
                    pool.wait_ge(f_wd, ev(1, i))
                    pool.sem_inc(s_pass, 1)
                    pool.tensor_copy(wdi[:, r:r + 1], wd[:, r, 0:1]).then_inc(f_wi, 1)
                    pool.wait_ge(f_wi, ev(1, i))
                    pool.wait_ge(f_yt, ev(1, i))
                    pool.sem_inc(s_pass, 1)
                    pool.indirect_dma_start(ys_d, bass.IndirectOffsetOnAxis(ap=wdi[:, r:r + 1], axis=0),
                                            yt[:, r, :], None).then_inc(f_sc[r], 16)
            for r in range(RT):
                pool.wait_ge(f_sc[r], 16 * (TILES // RT + 2))
            barrier(pool, 3)
            with pool.Fori(0, B // OB) as b4:
                for s in range(OB):
                    pool.wait_ge(o_in[s], 16 * K2 * (b4 + 1))
                    pool.tensor_tensor(er[:, s, 0], er[:, s, 0], er[:, s, 1], ALU.add).then_inc(o_a, 1)

        @block.scalar
        def _(act):
            start_ahead(act, (n_xn, 1), (n_xTh, 1), (n_sq, NJ), (e_uh, U), (e_Ah, 4),
                        (e_xn, 1), (e_xh, 1), (e_xTh, 1), (f_xTh, 1), (f_sl, 1))
            start_ahead(act, (e_z, 4), (f_yt, 1), spare=2)
            act.wait_ge(w_in[4], 16)
            act.activation(WNh[:, ROUTER:ROUTER + E], rwf[:], ACT.Copy).then_inc(s_rw, 1)
            place_of = {"q": 0, "k": 1024}
            for j, (kind, n) in enumerate(SETUP):
                act.wait_ge(s_tr, j + 1)
                o = place_of[kind] + 512 * n
                act.activation(WNh[:, o:o + 512], bank[j][:], ACT.Copy).then_inc(s_trh, 1)
            act.wait_ge(s_stat, 1)
            act.activation(t64[:, 1, :], t64[:, 0, :], ACT.Sqrt).then_inc(s_sqrt, 1)
            act.wait_ge(s_stat, 2)
            act.wait_ge(s_pool, 13)

            def normalised(dst, c, shift):
                return act.activation(dst, xa[:, bass.ds(c + 1, 1), :].rearrange("p a d -> p (a d)"), ACT.Identity,
                                      scale=rstd[:, bass.ds(c + 1, 1)], bias=shift[:, bass.ds(c + 1, 1)])

            def xn_norms(c, s):
                act.wait_ge(n_xT, ev(1, c - 2))
                normalised(xn[:, s, 0:D], c, nmr).then_inc(n_xn, 1)

            def xT_norms(c, s):
                act.wait_ge(n_xT, ev(1, c))
                act.wait_ge(n_qk, ev(NJ, c - 2, NJ - 1))
                act.activation(xTh[:, s, 0:P], bank[4 + s][:, 0:P], ACT.Copy).then_inc(n_xTh, 1)

            xn_norms(0, 0)
            xn_norms(1, 1)
            xT_norms(0, 0)
            with act.Fori(0, C // 2) as c2:
                for s in range(2):
                    c = c2 * 2 + s
                    for j in range(NJ):
                        act.wait_ge(n_qk, ev(NJ, c, j))
                        act.wait_ge(n_red, ev(NJ, c - 1, j))
                        act.activation(sq[:, j, 0:heads_width(j)], jbank[j][:, 0:heads_width(j)], ACT.Square).then_inc(n_sq, 1)
                        if j == 0:
                            xT_norms(c + 1, 1 - s)
                            xn_norms(c + 2, s)
            def late_out(j):
                kind, n = LATE[j]
                act.wait_ge(s_late, j + 1)
                if kind == "o":
                    dst = WoT[:, 4 * n:4 * n + 4, :]
                else:
                    dst = Mf[:, heads_of(n), :] if kind == "M" else Wx[:, heads_of(n), 0:D]
                act.activation(dst, bank[j % 4][:].rearrange("p (h d) -> p h d", d=D), ACT.Copy).then_inc(s_lateh, 1)

            for j in range(6):
                late_out(j)
            act.wait_ge(s_all, 1)
            act.activation(ra[:], mxa[:], ACT.Sqrt).then_inc(s_sqrt, 1)
            for j in range(6, len(LATE)):
                late_out(j)
            for g in range(U):
                act.wait_ge(s_Mt, g + 1)
                act.activation(Mh[0][:, 2 * g:2 * g + 2, :], Mt0[:, g % 2], ACT.Copy).then_inc(s_Mh, 1)
            act.wait_ge(s_rt, 1)
            act.activation(mm[:], mm[:], ACT.Exp).then_inc(s_sqrt, 1)
            barrier(act, 1)

            def for_scatter(c, s, p):
                act.wait_ge(c_out[s], 16 * K2 * p)
                normalised(pay[:, s, 0, 0:D], c, nmr)
                normalised(pay[:, s, 1, 0:D], c, nmr).then_inc(c_xn, 1)

            def normalise(c, r):
                act.wait_ge(a_G, ev(1, c - 4))
                act.wait_ge(e_xl, ev(1, c - 4))
                normalised(xn[:, r % 4], c, nmr1).then_inc(e_xn, 1)

            def x_hi(c, r):
                act.wait_ge(e_xn, ev(1, c))
                act.wait_ge(a_z, ev(4, c - 4, 3))
                act.activation(xh[:, r % 4], xn[:, r % 4], ACT.Copy).then_inc(e_xh, 1)

            def transposed(c, r):
                act.wait_ge(a_xT, ev(1, c))
                act.activation(xTh[:, r // 2 % 2, P * (r % 2):P * (r % 2) + P], wide("x", 2 + r % 2)[:, 0:P],
                               ACT.Copy).then_inc(e_xTh, 1)

            def u_hi(p, g):
                act.wait_ge(a_u, ev(U, p, g))
                act.wait_ge(a_z, ev(4, 2 * p - 1, g // 2))
                act.activation(uh[:, g].rearrange("p h i -> p (h i)"), wide("u", 0, g)[:], ACT.Identity,
                               bias=1.0 / D).then_inc(e_uh, 1)

            def scores_hi(c, q):
                act.wait_ge(e_Am, ev(4, c, q))
                act.wait_ge(a_z, ev(4, c - 1, q))
                act.activation(Ah[:, q], Am[:, q % 2], ACT.Copy).then_inc(e_Ah, 1)

            def z_out_(c, r, q):
                act.wait_ge(a_z, ev(4, c, q))
                act.wait_ge(a_Y, ev(4, c, q - 2) if q >= 2 else ev(4, c - 1, q + 2))
                act.activation(zf[:, q % 2], wide("z", r, q)[:].rearrange("p (h i) -> p h i", i=P), ACT.Copy).then_inc(e_z, 1)

            def attend_pair(p, pr):
                A, Z = 2 * p, 2 * p - 1
                u_hi(p, 0)
                u_hi(p, 1)
                z_out_(Z, -1, 2)
                u_hi(p, 2)
                u_hi(p, 3)
                u_hi(p, 4)
                scores_hi(A, 0)
                z_out_(Z, -1, 3)
                u_hi(p, 5)
                scores_hi(A, 1)
                u_hi(p, 6)
                z_out_(A, 0, 0)
                u_hi(p, 7)
                scores_hi(A, 2)
                normalise(A + 2, 2 * pr + 2)
                z_out_(A, 0, 1)
                scores_hi(A, 3)
                normalise(A + 3, 2 * pr + 3)
                x_hi(A + 2, 2 * pr + 2)
                scores_hi(A + 1, 0)
                z_out_(A, 0, 2)
                x_hi(A + 3, 2 * pr + 3)
                scores_hi(A + 1, 1)
                z_out_(A, 0, 3)
                transposed(A + 2, 2 * pr + 2)
                scores_hi(A + 1, 2)
                z_out_(A + 1, 1, 0)
                transposed(A + 3, 2 * pr + 3)
                for_scatter(A + 2, 0, p + 1)
                scores_hi(A + 1, 3)
                z_out_(A + 1, 1, 1)
                for_scatter(A + 3, 1, p + 1)

            for c in range(2):
                normalise(c, c)
            for c in range(2):
                transposed(c, c)
            for c in range(2):
                x_hi(c, c)
            for s in range(2):
                normalised(pay[:, s, 0, 0:D], s, nmr)
                normalised(pay[:, s, 1, 0:D], s, nmr).then_inc(c_xn, 1)
            with act.Fori(0, C // 4) as c4:
                for pr in range(2):
                    attend_pair(c4 * 2 + pr, pr)
            z_out_(C - 1, -1, 2)
            z_out_(C - 1, -1, 3)
            act.preload_act_table(ACT.Silu)
            barrier(act, 2)

            act.wait_ge(f_w, 32)
            for e in (*range(E - 3, E), *range(E - 3)):
                act.activation(guh[:, e], gu[:, e], ACT.Copy).then_inc(f_wh, 1)

            def tile_hi(i, s):
                act.wait_ge(f_xT, ev(1, i))
                act.wait_ge(f_u, ev(1, i - 2))
                act.activation(xtTh[:, s, :], bank[0][:, 0:P], ACT.Copy).then_inc(f_xTh, 1)

            def result(i, r, s, uses):
                act.wait_ge(f_y, ev(1, i))
                act.wait_ge(f_sc[r], 16 * uses)
                act.activation(yt[:, r, :], bank[6 + s][:, 0:D], ACT.Copy, scale=wd[:, r, 1:2]).then_inc(f_yt, 1)

            tile_hi(0, 0)
            with act.Fori(0, TILES // RT) as i4:
                for r in range(RT):
                    i, s = i4 * RT + r, r % 2
                    tile_hi(i + 1, 1 - s)
                    act.wait_ge(f_g, ev(1, i))
                    act.wait_ge(f_act, ev(1, i - 2))
                    act.activation(sl[:, s, :], bank[1 + s][:, 0:F], ACT.Silu).then_inc(f_sl, 1)
                    result(i - 2, (r - 2) % RT, s, i4 + 2 if r >= 2 else i4 + 1)
            result(TILES - 2, RT - 2, 0, TILES // RT + 1)
            result(TILES - 1, RT - 1, 1, TILES // RT + 1)
            barrier(act, 3)
            with act.Fori(0, B // OB) as b4:
                for s in range(OB):
                    b = b4 * OB + s
                    act.wait_ge(o_b, ev(1, b))
                    act.dma_start(out[bass.ds(b * CB, CB)].rearrange("c p d -> p c d"), ot[:, s]).then_inc(o_out[s], 16)

        @block.vector
        def _(dve):
            start_ahead(dve, (n_xTl, 1), (n_red, NJ), (n_lc, 1), (e_ul, U), (e_Am, 4), (e_G, 1), (e_Gs, 1),
                        (e_xTl, 1), (f_xTl, 1), (f_wd, 1), (f_act, 1), (o_b, 1))
            start_ahead(dve, (e_r, 4), (e_Y, 4), spare=3)
            start_ahead(dve, (f_aTc, 1), spare=1)
            links = [0]

            def link(ins):
                links[0] += 1
                ins.then_inc(s_chain, 1)
                dve.wait_ge(s_chain, links[0])

            def rsqrt(dst, val, root, tmp):
                link(dve.reciprocal(dst, root))
                link(dve.tensor_tensor(tmp, dst, dst, ALU.mult))
                link(dve.tensor_tensor(tmp, tmp, val, ALU.mult))
                link(dve.tensor_scalar(tmp, tmp, -0.5, 1.5, ALU.mult, ALU.add))
                link(dve.tensor_tensor(dst, dst, tmp, ALU.mult))

            def centre(n, t):
                dve.wait_ge(w_in[n], 16)
                link(dve.tensor_reduce(wmean[:, n, :], t[:], AX.X, ALU.add))
                link(dve.tensor_scalar(wmean[:, n, :], wmean[:, n, :], 1.0 / D, None, ALU.mult))
                dve.tensor_tensor(t[:], t[:], wmean[:, n, :].unsqueeze(2).broadcast_to([P, 8, D]),
                                  ALU.subtract).then_inc(s_ctr, 1)

            centre(0, wqn)
            centre(1, wkn)
            def weights_lo(j):
                kind, n = SETUP[j]
                o = (1024 if kind == "k" else 0) + 512 * n
                dve.wait_ge(s_trh, j + 1)
                dve.tensor_tensor(WNl[:, o:o + 512], bank[j][:], WNh[:, o:o + 512], ALU.subtract).then_inc(s_trl, 1)

            dve.wait_ge(s_rw, 1)
            dve.tensor_tensor(WNl[:, ROUTER:ROUTER + E], rwf[:], WNh[:, ROUTER:ROUTER + E], ALU.subtract).then_inc(s_trl, 1)
            for n in range(B + 1):
                if n < B:
                    dve.wait_ge(x_in[n], 16)
                    for c in range(n * CB, n * CB + CB):
                        dve.bn_stats(eqw[:, c, 0:6], xa[:, c + 1, :]).then_inc(s_bs, 1)
                if n > 0:
                    dve.wait_ge(s_bs, n * CB)
                    for c in range((n - 1) * CB, n * CB):
                        links[0] += 1
                        dve.bn_aggr(mv[:, c, :], eqw[:, c, 0:6]).then_inc(s_chain, 1)
                if 4 <= n < 8:
                    weights_lo(n - 4)
            dve.wait_ge(s_chain, links[0])
            dve.tensor_scalar(t64[:, 0, :], mv[:, :, 1], EPS, None, ALU.add).then_inc(s_stat, 1)
            dve.wait_ge(s_sqrt, 1)
            rsqrt(rstd[:, 1:C + 1], t64[:, 0, :], t64[:, 1, :], mm[:])
            dve.scalar_tensor_tensor(nmr[:, 1:C + 1], mv[:, :, 0], -1.0, rstd[:, 1:C + 1], ALU.mult, ALU.mult).then_inc(s_stat, 1)
            dve.wait_ge(s_stat, 2)
            dve.tensor_scalar(nmr1[:, 1:C + 1], nmr[:, 1:C + 1], 1.0, None, ALU.add).then_inc(s_stat, 1)

            def xTl_norms(c, s):
                dve.wait_ge(n_xTh, ev(1, c))
                dve.tensor_tensor(xTl[:, s, 0:P], bank[4 + s][:, 0:P], xTh[:, s, 0:P], ALU.subtract).then_inc(n_xTl, 1)

            xTl_norms(0, 0)
            centre(2, wvn)
            with dve.Fori(0, C // 2) as c2:
                for s in range(2):
                    c = c2 * 2 + s
                    for j in range(NJ):
                        dve.wait_ge(n_sq, ev(NJ, c, j))
                        if j == NJ - 1:
                            dve.tensor_copy(L[:, bass.ds(c, 1), :].rearrange("p a e -> p (a e)"),
                                            jbank[j][:, heads_width(j):heads_width(j) + E]).then_inc(n_lc, 1)
                        dve.tensor_reduce(ssq[:, bass.ds(c, 1), job_heads(j)].rearrange("p a h -> p (a h)"),
                                          sq[:, j, 0:heads_width(j)].rearrange("p (h e) -> p h e", e=DH),
                                          AX.X, ALU.add).then_inc(n_red, 1)
                        if j == 0:
                            xTl_norms(c + 1, 1 - s)
            dve.wait_ge(n_red, ev(NJ, C - 1, NJ - 1))
            dve.wait_ge(n_lc, ev(1, C - 1))
            dve.tensor_reduce(mx[:], ssq[:].rearrange("p (b c) h -> p b h c", b=B), AX.X, ALU.max).then_inc(s_mx, 1)

            bc = [P, C, E]
            link(dve.tensor_reduce(m1[:], L[:], AX.X, ALU.max))

            def first_of(best, src, k):
                link(dve.tensor_tensor(eqw[:], src[:], best[:].unsqueeze(2).broadcast_to(bc), ALU.is_equal))
                link(dve.tensor_tensor(eqw[:], eqw[:], ord8[:].unsqueeze(1).broadcast_to(bc), ALU.mult))
                link(dve.tensor_reduce(slf[:, 0:C], eqw[:], AX.X, ALU.max))
                link(dve.tensor_tensor(oh[:, k], ord8[:].unsqueeze(1).broadcast_to(bc),
                                       slf[:, 0:C].unsqueeze(2).broadcast_to(bc), ALU.is_equal))
                dve.tensor_copy(ohb[:, k], oh[:, k]).then_inc(r_oh, 1)

            dve.wait_ge(s_const, 9)
            first_of(m1, L, 0)
            dve.wait_ge(s_sqrt, 2)
            rsqrt(rb[:], mxa[:], ra[:], mx[:])
            link(dve.tensor_tensor(cc[:, 0:B, :], rb[:, :, 0:H], rb[:, :, H:2 * H], ALU.mult))
            dve.sem_inc(s_cc, 1)
            link(dve.scalar_tensor_tensor(L2[:].rearrange("p c e -> p (c e)"),
                                          oh[:, 0].rearrange("p c e -> p (c e)"), -3.0e38,
                                          L[:].rearrange("p c e -> p (c e)"), ALU.mult, ALU.add))
            link(dve.tensor_reduce(m2[:], L2[:], AX.X, ALU.max))
            first_of(m2, L2, 1)
            dve.tensor_tensor(mm[:], m2[:], m1[:], ALU.subtract).then_inc(s_rt, 1)
            link(dve.memset(pre[:, 0, :], 0.0))
            dve.wait_ge(r_cnt, 1)
            for k in range(K2):
                for e in range(E):
                    first = 0.0 if k == 0 else pre[:, C, e:e + 1]
                    links[0] += 1
                    dve.tensor_tensor_scan(pre[:, k * C + 1:(k + 1) * C + 1, e], onesf[:, 0:C],
                                                bank[2 + k][:].rearrange("p (c e) -> p c e", e=E)[:, :, e],
                                                first, ALU.mult, ALU.add).then_inc(s_chain, 1)
                dve.wait_ge(s_chain, links[0])
            link(dve.tensor_copy(cnt[:], pre[:, K2 * C, :]))
            link(dve.tensor_scalar(til[:], cnt[:], float(P - 1), None, ALU.add))
            link(dve.tensor_copy(cnti[:], til[:]))
            link(dve.tensor_single_scalar(cnti[:], cnti[:], 7, ALU.logical_shift_right))
            link(dve.tensor_copy(til[:], cnti[:]))
            link(dve.tensor_tensor_scan(endt[:], onesf[:, 0:E], til[:], 0.0, ALU.mult, ALU.add))
            link(dve.tensor_tensor(base[:], endt[:], til[:], ALU.subtract))
            link(dve.tensor_scalar(base[:], base[:], float(P), float(P), ALU.mult, ALU.add))
            link(dve.tensor_scalar(padf[:], endt[:], float(P), iop[:, 0:1], ALU.mult, ALU.add))
            link(dve.tensor_copy(pad[:], padf[:]))
            dve.sem_inc(s_pad, 1)
            for k in range(K2):
                kc = slice(k * C, (k + 1) * C)
                link(dve.tensor_tensor(posn[:, kc], pre[:, kc], bank[k][:].rearrange("p (c e) -> p c e", e=E), ALU.add))
            link(dve.tensor_tensor(posn[:], posn[:], base[:].unsqueeze(1).broadcast_to([P, K2 * C, E]), ALU.add))
            link(dve.tensor_tensor(posn[:], posn[:], oh[:].rearrange("p k c e -> p (k c) e"), ALU.mult))
            link(dve.tensor_reduce(slf[:], posn[:], AX.X, ALU.add))
            link(dve.tensor_copy(slot[:].rearrange("p c k -> p k c"), slf[:].rearrange("p (k c) -> p k c", k=K2)))
            dve.wait_ge(s_sqrt, 3)
            link(dve.tensor_scalar(m1[:], mm[:], 1.0, None, ALU.add))
            link(dve.reciprocal(wtop[:, 0, :], m1[:]))
            link(dve.tensor_tensor(wtop[:, 1, :], wtop[:, 0, :], mm[:], ALU.mult))
            link(dve.tensor_copy(meta[:, :, :, 1], wtop[:].rearrange("p k c -> p c k")))
            barrier(dve, 1)

            def transposed_lo(c, r):
                t = slice(P * (r % 2), P * (r % 2) + P)
                dve.wait_ge(e_xTh, ev(1, c))
                dve.tensor_tensor(xTl[:, r // 2 % 2, t], wide("x", 2 + r % 2)[:, 0:P],
                                  xTh[:, r // 2 % 2, t], ALU.subtract).then_inc(e_xTl, 1)

            def u_lo(p, g):
                dve.wait_ge(e_uh, ev(U, p, g))
                dve.scalar_tensor_tensor(ul[:, g].rearrange("p h i -> p (h i)"), wide("u", 0, g)[:], 1.0 / D,
                                         uh[:, g].rearrange("p h i -> p (h i)"), ALU.add, ALU.subtract).then_inc(e_ul, 1)

            def mask(c, s, q):
                dve.wait_ge(a_s, ev(4, c, q))
                dve.wait_ge(e_Al, ev(4, c, q - 2) if q >= 2 else ev(4, c - 1, q + 2))
                dve.tensor_tensor(Am[:, q % 2], wide("s", s, q)[:].rearrange("p (h i) -> p h i", i=P),
                                  causal[:].unsqueeze(1).broadcast_to([P, HQ, P]), ALU.mult).then_inc(e_Am, 1)

            def ys(q):
                return ybank[q % 2][:, :, 0:2 * VE].rearrange("p b (h e) -> p b h e", e=VE)

            def inverse(c, q):
                dve.wait_ge(a_Y, ev(4, c, q))
                dve.reciprocal(rden[:, q], ys(q)[:, :, :, D]).then_inc(e_r, 1)

            def weigh(c, s, q):
                dve.wait_ge(e_r, ev(4, c, q))
                if q == 0:
                    dve.wait_ge(e_sum, ev(1, c - 2))
                else:
                    dve.wait_ge(e_Y, ev(4, c, q - 1))
                for i in range(HQ):
                    y_, d_ = ys(q)[:, i // 2, i % 2, 0:D], rden[:, q, i // 2, i % 2:i % 2 + 1]
                    if q == 0 and i > 1:
                        last = dve.tensor_scalar(acc[:, s, i], y_, d_, None, ALU.mult)
                    else:
                        before_ = acc[:, s, i]
                        if q == 0:
                            before_ = bob[:] if i == 1 else xa[:, bass.ds(c + 1, 1), :].rearrange("p a d -> p (a d)")
                        last = dve.scalar_tensor_tensor(acc[:, s, i], y_, d_, before_, ALU.mult, ALU.add)
                last.then_inc(e_Y, 1)

            def G_add(c, s):
                dve.wait_ge(a_G, ev(1, c))
                dve.tensor_tensor(Gf[:], wide("G", s)[:, 0:D], Gf[:], ALU.add).then_inc(e_G, 1)

            def G_split(c, s):
                dve.wait_ge(e_G, ev(1, c))
                dve.wait_ge(a_z, ev(4, c - 1, 3))
                dve.tensor_copy(Gh[:, 1 - s], Gf[:]).then_inc(s_gh, 1)
                dve.wait_ge(s_gh, c + 1)
                dve.tensor_tensor(Gl[:, 1 - s], Gf[:], Gh[:, 1 - s], ALU.subtract).then_inc(e_Gs, 1)

            transposed_lo(0, 0)
            transposed_lo(1, 1)
            for t, v in ((Gf[:], 0.0), (Gh[:].bitcast(f32), 0.0), (Gl[:].bitcast(f32), 0.0), (Wx[:, :, D:VE], 1.0 / D),
                         (xh[:, 3].bitcast(f32), 1.0), (xl[:, 3].bitcast(f32), 0.0),
                         (Ah[:, 2:4].bitcast(f32), 1.0), (uh[:, 4:8, :, P:2 * P].bitcast(f32), 0.0),
                         (acc[:, 1], 0.0)):
                dve.memset(t, v).then_inc(s_dummy, 1)
            dve.wait_ge(s_dummy, 12)
            dve.sem_inc(e_Gs, 1)
            with dve.Fori(0, B) as b:
                with dve.Fori(0, CB // 4) as half:
                    for pr in range(2):
                        p = b * (CB // 2) + half * 2 + pr
                        A, Z = 2 * p, 2 * p - 1
                        u_lo(p, 0)
                        u_lo(p, 1)
                        u_lo(p, 2)
                        inverse(Z, 1)
                        u_lo(p, 3)
                        mask(A, 0, 0)
                        u_lo(p, 4)
                        weigh(Z, 1, 1)
                        u_lo(p, 5)
                        inverse(Z, 2)
                        mask(A, 0, 1)
                        weigh(Z, 1, 2)
                        u_lo(p, 6)
                        inverse(Z, 3)
                        u_lo(p, 7)
                        mask(A, 0, 2)
                        weigh(Z, 1, 3)
                        G_add(A, 0)
                        inverse(A, 0)
                        mask(A, 0, 3)
                        weigh(A, 0, 0)
                        G_split(A, 0)
                        mask(A + 1, 1, 0)
                        inverse(A, 1)
                        mask(A + 1, 1, 1)
                        weigh(A, 0, 1)
                        inverse(A, 2)
                        transposed_lo(A + 2, 2 * pr + 2)
                        mask(A + 1, 1, 2)
                        weigh(A, 0, 2)
                        inverse(A, 3)
                        G_add(A + 1, 1)
                        weigh(A, 0, 3)
                        transposed_lo(A + 3, 2 * pr + 3)
                        mask(A + 1, 1, 3)
                        G_split(A + 1, 1)
                        inverse(A + 1, 0)
                        weigh(A + 1, 1, 0)
                dve.wait_ge(e_Gs, ev(1, b * CB + CB))
                dve.memset(Gf[:], 0.0).then_inc(s_new, 1)
                dve.wait_ge(s_new, b + 1)
            for q in range(1, Q):
                inverse(C - 1, q)
                weigh(C - 1, 1, q)
            barrier(dve, 2)

            link(dve.memset(tile_e[:], 0))
            link(dve.tensor_tensor(ge[:], iot[:].unsqueeze(2).broadcast_to([P, TILES, E]),
                                   endt[:].unsqueeze(1).broadcast_to([P, TILES, E]), ALU.is_ge))
            link(dve.tensor_reduce(tef[:], ge[:], AX.X, ALU.add))
            link(dve.tensor_scalar(tef[:], tef[:], float(E - 1), None, ALU.min))
            dve.tensor_copy(tile_e[:, 2:TILES + 2], tef[:]).then_inc(f_te, 1)
            for e in range(E - 3):
                dve.wait_ge(f_wh, e + 4)
                dve.tensor_tensor(gul[:, e], gu[:, e], guh[:, e], ALU.subtract).then_inc(f_wl, 1)

            def tile_lo(i, s):
                dve.wait_ge(f_xTh, ev(1, i))
                dve.tensor_tensor(xtTl[:, s, :], bank[0][:, 0:P], xtTh[:, s, :], ALU.subtract).then_inc(f_xTl, 1)

            def tile_meta(i, r):
                dve.wait_ge(f_wi, ev(1, i - RT))
                dve.wait_ge(f_yt, ev(1, i - RT))
                dve.tensor_copy(wd[:, r, :], xt[:, r, D:D + 2]).then_inc(f_wd, 1)

            def hidden_out(i, s):
                dve.wait_ge(f_aT, ev(1, i))
                dve.wait_ge(f_y, ev(1, i - 2))
                dve.tensor_copy(aT[:, s].rearrange("p t i -> p (t i)"), bank[5][:, 0:FT * P]).then_inc(f_aTc, 1)

            dve.wait_ge(f_ms, 3)
            tile_lo(0, 0)
            tile_meta(0, 0)
            with dve.Fori(0, TILES // RT) as i4:
                for r in range(RT):
                    i, s = i4 * RT + r, r % 2
                    tile_lo(i + 1, 1 - s)
                    tile_meta(i + 1, (r + 1) % RT)
                    hidden_out(i - 1, 1 - s)
                    dve.wait_ge(f_sl, ev(1, i))
                    dve.wait_ge(f_u, ev(1, i))
                    dve.wait_ge(f_aT, ev(1, i - 2))
                    dve.tensor_tensor(act_[:, s, 0:F], bank[3 + s][:, 0:F], sl[:, s, :], ALU.mult).then_inc(f_act, 1)
            hidden_out(TILES - 1, 1)
            barrier(dve, 3)
            with dve.Fori(0, B // OB) as b4:
                for s in range(OB):
                    b = b4 * OB + s
                    dve.wait_ge(o_out[s], 16 * (b4 + 1))
                    dve.wait_ge(o_a, ev(1, b))
                    dve.tensor_tensor(ot[:, s], er[:, s, 0], xa[:, bass.ds(b * CB + 1, CB), :], ALU.add).then_inc(o_b, 1)

        @block.tensor
        def _(pe):
            start_ahead(pe, (n_xT, 1), (n_qk, NJ), (a_u, U), (a_s, 4), (a_G, 1),
                        (a_xT, 1), (f_xT, 1), (f_g, 1), (f_u, 1))
            start_ahead(pe, (f_aT, 1), spare=1)
            start_ahead(pe, (a_z, 4), (f_y, 1), spare=2)
            start_ahead(pe, (a_Y, 4), spare=3)

            def split3(dst, ah, al, bh, bl, start=True, stop=True):
                pe.matmul(dst, ah, bh, start=start, stop=False)
                pe.matmul(dst, al, bh, start=False, stop=False)
                return pe.matmul(dst, ah, bl, start=False, stop=stop)

            pe.wait_ge(s_const, 1)
            pe.wait_ge(s_ctr, 2)
            natural = {"q": wqn, "k": wkn, "o": won}

            def transpose4(dst, kind, n):
                for i in range(4):
                    last = pe.transpose(dst[:, P * i:P * i + P], natural[kind][:, 4 * n + i, :], ident[:])
                return last

            for j, (kind, n) in enumerate(SETUP):
                transpose4(bank[j], kind, n).then_inc(s_tr, 1)
            pe.wait_ge(s_trh, len(SETUP))
            pe.wait_ge(s_trl, len(SETUP) + 1)

            def xT_for_norms(c, s):
                pe.wait_ge(n_xn, ev(1, c))
                pe.wait_ge(n_xTl, ev(1, c - 2))
                pe.transpose(bank[4 + s][:, 0:P], xn[:, s, 0:D], ident[:]).then_inc(n_xT, 1)

            xT_for_norms(0, 0)
            with pe.Fori(0, C // 2) as c2:
                for s in range(2):
                    c = c2 * 2 + s
                    pe.wait_ge(n_xTl, ev(1, c))
                    for j in range(NJ):
                        pe.wait_ge(n_sq, ev(NJ, c - 1, j))
                        if j == NJ - 1:
                            pe.wait_ge(n_lc, ev(1, c - 1))
                        w = job_columns(j)
                        split3(jbank[j][:, 0:w.stop - w.start], xTh[:, s, 0:P], xTl[:, s, 0:P],
                               WNh[:, w], WNl[:, w]).then_inc(n_qk, 1)
                        if j == 0:
                            xT_for_norms(c + 1, 1 - s)
            pe.wait_ge(n_sq, ev(NJ, C - 1, NJ - 1))
            pe.wait_ge(w_in[3], 16)
            pe.wait_ge(s_ctr, 3)
            for j, (kind, n) in enumerate(LATE):
                if j >= 4:
                    pe.wait_ge(s_lateh, j - 3)
                dst = bank[j % 4]
                if kind == "o":
                    last = transpose4(dst, "o", n)
                else:
                    if kind == "W":
                        pe.wait_ge(s_lateh, 6)
                    left, right = (wqn, wkn) if kind == "M" else (wvn, WoT)
                    for i in range(4):
                        h = heads_of(n).start + 2 * i
                        r = slice(DH * (h % 2), DH * (h % 2) + DH)
                        last = pe.matmul(dst[:, P * i:P * i + P], left[r, h // 2, :], right[r, h // 2, :], start=True, stop=True)
                last.then_inc(s_late, 1)
            pe.wait_ge(s_lateh, len(LATE))
            pe.wait_ge(r_oh, 2)
            pe.wait_ge(n_sq, ev(NJ, C - 1, NJ - 1))
            for k in range(K2):
                pe.matmul(bank[k][:], before[:], ohb[:, k].rearrange("p c e -> p (c e)"), start=True, stop=True)
                last = pe.matmul(bank[2 + k][:], ones[:], ohb[:, k].rearrange("p c e -> p (c e)"), start=True, stop=True)
            last.then_inc(r_cnt, 1)
            barrier(pe, 1)

            def transpose_x(c, r, p=None):
                if p is not None:
                    wait_wide(pe, p, "x", 2 + r % 2)
                pe.wait_ge(e_xn, ev(1, c))
                pe.transpose(wide("x", 2 + r % 2)[:, 0:P], xn[:, r % 4], ident[:]).then_inc(a_xT, 1)

            def u(p, pr, b, bp, g):
                wait_wide(pe, p, "u", 0, g)
                pe.wait_ge(e_M, ev(U, b, g))
                for n in range(2):
                    last = split3(wide("u", 0, g)[:, 2 * P * n:2 * P * n + 2 * P],
                                  Mh[bp][:, 2 * g + n, :], Ml[bp][:, 2 * g + n, :], xTh[:, pr, :], xTl[:, pr, :])
                last.then_inc(a_u, 1)

            def scores(p, pr, s, q):
                wait_wide(pe, p, "s", s, q)
                pe.wait_ge(e_ul, ev(U, p, 2 * q + 1))
                t = slice(P * s, P * s + P)
                split3(wide("s", s, q)[:].rearrange("p (h i) -> p h i", i=P), xTh[:, pr, t], xTl[:, pr, t],
                       uh[:, 2 * q:2 * q + 2, :, t].rearrange("p g h i -> p (g h) i"),
                       ul[:, 2 * q:2 * q + 2, :, t].rearrange("p g h i -> p (g h) i")).then_inc(a_s, 1)

            def z(p, r, x_slot, q, first=False, last=False):
                c, s = 2 * p + r, r % 2
                if last:
                    pe.wait_ge(e_z, ev(4, c, 1))
                else:
                    wait_wide(pe, p, "z", r, q)
                if r < 0:
                    pe.wait_ge(s_dummy, 12)
                else:
                    pe.wait_ge(e_xl, ev(1, c))
                    pe.wait_ge(e_Gs, ev(1, c))
                pe.wait_ge(e_Al, ev(4, c, q))
                dst = wide("z", r, q)[:].rearrange("p (h i) -> p h i", i=P)
                t = slice(P * s, P * s + P)
                if not first:
                    split3(dst, Gh[:, s], Gl[:, s],
                           uh[:, 2 * q:2 * q + 2, :, t].rearrange("p g h i -> p (g h) i"),
                           ul[:, 2 * q:2 * q + 2, :, t].rearrange("p g h i -> p (g h) i"), stop=False)
                split3(dst, xh[:, x_slot], xl[:, x_slot], Ah[:, q], Al[:, q], start=first).then_inc(a_z, 1)

            def Y(c, q):
                pe.wait_ge(e_Y, ev(4, c, q - 2) if q >= 2 else ev(4, c - 1, q + 2))
                pe.wait_ge(e_z, ev(4, c, q))
                for i in range(HQ):
                    last = pe.matmul(ybank[q % 2][:, i // 2, VE * (i % 2):VE * (i % 2) + VE], zf[:, q % 2, i, :],
                                     Wx[:, HQ * q + i, :], start=True, stop=True)
                last.then_inc(a_Y, 1)

            def G(p, pr, s):
                wait_wide(pe, p, "G", s)
                x_ = xn[:, 2 * pr + s]
                pe.matmul(wide("G", s)[:, 0:D], x_, x_, start=True, stop=True).then_inc(a_G, 1)

            def attend_pair(p, pr, b, bp, first):
                A, Z, z_slot = 2 * p, 2 * p - 1, (2 * pr - 1) % 4
                pe.wait_ge(e_xTl, ev(1, A + 1))
                u(p, pr, b, bp, 0)
                u(p, pr, b, bp, 1)
                z(p, -1, z_slot, 2)
                u(p, pr, b, bp, 2)
                Y(Z, 1)
                u(p, pr, b, bp, 3)
                scores(p, pr, 0, 0)
                u(p, pr, b, bp, 4)
                z(p, -1, z_slot, 3)
                u(p, pr, b, bp, 5)
                Y(Z, 2)
                scores(p, pr, 0, 1)
                u(p, pr, b, bp, 6)
                z(p, 0, 2 * pr, 0, first)
                u(p, pr, b, bp, 7)
                Y(Z, 3)
                scores(p, pr, 0, 2)
                G(p, pr, 0)
                z(p, 0, 2 * pr, 1, first)
                scores(p, pr, 0, 3)
                Y(A, 0)
                scores(p, pr, 1, 0)
                z(p, 0, 2 * pr, 2, first)
                Y(A, 1)
                scores(p, pr, 1, 1)
                z(p, 0, 2 * pr, 3, first)
                transpose_x(A + 2, 2 * pr + 2, p)
                Y(A, 2)
                scores(p, pr, 1, 2)
                z(p, 1, 2 * pr + 1, 0)
                transpose_x(A + 3, 2 * pr + 3, p)
                G(p, pr, 1)
                Y(A, 3)
                scores(p, pr, 1, 3)
                z(p, 1, 2 * pr + 1, 1)
                Y(A + 1, 0)

            transpose_x(0, 0)
            transpose_x(1, 1)
            with pe.Fori(0, B // 2) as b2:
                for bp in range(2):
                    b = b2 * 2 + bp
                    for n in range(CB // 2):
                        attend_pair(b * (CB // 2) + n, n % 2, b, bp, n == 0)
            z(C // 2, -1, 3, 2)
            Y(C - 1, 1)
            z(C // 2, -1, 3, 3, last=True)
            Y(C - 1, 2)
            Y(C - 1, 3)
            barrier(pe, 2)


            expert_reg = [pe.alloc_register(f"expert{n}") for n in range(4)]

            def load_expert(i, r):
                pe.reg_load(expert_reg[r % 4], tile_e[0:1, bass.ds(i + 2, 1)])

            def tile_expert(r):
                return pe.snap(expert_reg[r % 4], min_val=0, max_val=E - 1)

            def transpose_tile(i, r):
                pe.wait_ge(f_xTl, ev(1, i - 1))
                pe.transpose(bank[0][:, 0:P], xt[:, r, 0:D], ident[:]).then_inc(f_xT, 1)

            def gate_up(i, s, ex, g, free, done):
                pe.wait_ge(free, ev(1, i - 2))
                wh = guh[:, bass.ds(ex, 1), g, :].rearrange("p a f -> p (a f)")
                wl = gul[:, bass.ds(ex, 1), g, :].rearrange("p a f -> p (a f)")
                split3(bank[1 + 2 * g + s][:, 0:F], xtTh[:, s, :], xtTl[:, s, :], wh, wl).then_inc(done, 1)

            def transpose_hidden(i, s):
                pe.wait_ge(f_act, ev(1, i))
                pe.wait_ge(f_aTc, ev(1, i - 1))
                for t in range(FT):
                    last = pe.transpose(bank[5][:, P * t:P * t + P], act_[:, s, P * t:P * t + P], ident[:])
                last.then_inc(f_aT, 1)

            def down_(i, s, ex):
                pe.wait_ge(f_aTc, ev(1, i))
                pe.wait_ge(f_yt, ev(1, i - 2))
                for t in range(FT):
                    last = pe.matmul(bank[6 + s][:, 0:D], aT[:, s, t, :], dn[:, bass.ds(ex, 1), t, :].rearrange("p a f -> p (a f)"),
                                     start=(t == 0), stop=(t == FT - 1))
                last.then_inc(f_y, 1)

            pe.wait_ge(f_xt[0], 16)
            transpose_tile(0, 0)
            pe.wait_ge(f_ms, 3)
            pe.wait_ge(f_te, 1)
            for n in (-2, -1, 0):
                load_expert(n, n)
            pe.wait_ge(f_wl, E)
            pe.wait_ge(f_dn, 32 * E)
            with pe.Fori(0, TILES // RT) as i4:
                ex2, ex1 = tile_expert(-2), tile_expert(-1)
                for r in range(RT):
                    i, s = i4 * RT + r, r % 2
                    ex = tile_expert(r)
                    pe.wait_ge(f_xTl, ev(1, i))
                    gate_up(i, s, ex, 0, f_sl, f_g)
                    pe.wait_ge(f_xt[(r + 1) % RT], 16 * (i4 + 1) if r < RT - 1 else 16 * (i4 + 2))
                    transpose_tile(i + 1, (r + 1) % RT)
                    transpose_hidden(i - 1, 1 - s)
                    gate_up(i, s, ex, 1, f_act, f_u)
                    load_expert(i + 1, r + 1)
                    down_(i - 2, s, ex2)
                    ex2, ex1 = ex1, ex
            transpose_hidden(TILES - 1, 1)
            for n in (TILES - 2, TILES - 1):
                down_(n, n % 2, tile_expert(n))
            barrier(pe, 3)


_INS = ["L0_attn_X", "L0_attn_Wq", "L0_attn_Wk", "L0_attn_Wv", "L0_attn_Wo", "L0_attn_bo",
        "L0_ffn_router_w", "L0_ffn_gate_proj", "L0_ffn_up_proj", "L0_ffn_down_proj"]


def kernel(**inputs):
    import numpy as np
    import concourse.bacc as bacc
    from concourse import mybir as mb
    from concourse.bass_utils import run_bass_kernel_spmd as run

    nc = bacc.Bacc("TRN2", target_bir_lowering=False, num_devices=1)
    arrays, args = {}, []
    for name in _INS:
        a = np.ascontiguousarray(inputs[name])
        arrays[f"in_{name}"] = a
        args.append(nc.dram_tensor(f"in_{name}", a.shape, mb.dt.from_np(a.dtype), kind="ExternalInput").ap())
    args.append(nc.dram_tensor("out_0", (C, P, D), mb.dt.float32, kind="ExternalOutput").ap())
    build(nc, *args)
    r = run(nc, [arrays], core_ids=[0])
    return r.results[0]["out_0"].reshape(B, N, D)
```
